# Optimizing a Trainium2 kernel written in Bass

```python
import numpy as np
import jax
import jax.numpy as jnp

def _softmax(x, axis=-1):
    return jax.nn.softmax(x, axis=axis)

def _gelu(x):
    return jax.nn.gelu(x, approximate=True)

def _silu(x):
    return jax.nn.silu(x)

def _sigmoid(x):
    return jax.nn.sigmoid(x)

def _layernorm(x, axis=-1, eps=1e-05):
    m = jnp.mean(x, axis=axis, keepdims=True)
    v = jnp.var(x, axis=axis, keepdims=True)
    return (x - m) / jnp.sqrt(v + eps)

def _scatter_add(tgt, idx, src, axis=0):
    return tgt.at[idx].add(src)

def _segment_sum(src, seg, n):
    return jax.ops.segment_sum(src, seg, n)
kernel_name = 'mk_decoder_postln_d2_seqx_r8_2c93b4'

def setup_inputs(seed: int=0):
    np.random.seed(seed)
    _w = jnp.asarray

    def _rec_inputs():
        import jax
        import jax.numpy as jnp
        _rk = jax.random.key(seed)
        x = 0.0002279 + 0.9999 * jax.random.normal(jax.random.fold_in(_rk, 1), (16, 128, 128), jnp.float32)
        _lenS = 128 - jax.random.randint(jax.random.fold_in(_rk, 7), (16,), 0, max(1, 128 // 4) + 1, jnp.int32)
        _lenS2 = 77 - jax.random.randint(jax.random.fold_in(_rk, 8), (16,), 0, max(1, 77 // 4) + 1, jnp.int32)
        _ctx_1024P = jax.random.normal(jax.random.fold_in(_rk, 11), (16, 16, 128), jnp.float32)
        _ctx_1024c = jax.random.dirichlet(jax.random.fold_in(_rk, 511), 0.3 * jnp.ones((16,), jnp.float32), (16, 77))
        _ctx_1024t = jnp.einsum('bsk,bkd->bsd', _ctx_1024c, _ctx_1024P)
        _ctx_1024t = _ctx_1024t * jax.lax.rsqrt(jnp.mean(jnp.square(_ctx_1024t)) + 1e-12) * 0.953939
        ctx_1024 = -0.000392918 + 0.999932 * (_ctx_1024t + 0.3 * jax.random.normal(jax.random.fold_in(_rk, 611), (16, 77, 128), jnp.float32))
        fside_Bx16_0 = 0.119436 + 0.907674 * jax.random.normal(jax.random.fold_in(_rk, 12), (16, 16), jnp.float32)
        return (x, ctx_1024, fside_Bx16_0)
    x, ctx_1024, fside_Bx16_0 = _rec_inputs()

    def _L0_attn_setup():
        import jax, jax.numpy as jnp
        import numpy as np
        B, S, D, H = (4, 256, 128, 16)
        HD = D // H
        LN_EPS = 1e-05
        KERN_EPS = 1e-06

        def kernel_func(q, k):
            scores = jnp.einsum('bhqd,bhkd->bhqk', q, k) / jnp.sqrt(jnp.asarray(HD, q.dtype))
            w = jax.nn.relu(scores)
            return w / (jnp.sum(w, axis=-1, keepdims=True) + KERN_EPS)
        key = jax.random.key(seed)
        k1, k2, k3 = jax.random.split(key, 3)
        scale = 1.0 / np.sqrt(D)
        return {'x': jax.random.normal(k1, (B, S, D), dtype=jnp.float32), 'w_qkv': jax.random.normal(k2, (D, 3 * D), dtype=jnp.float32) * scale, 'w_out': jax.random.normal(k3, (D, D), dtype=jnp.float32) * scale, 'b_out': jnp.zeros((D,), dtype=jnp.float32), 'gamma': jnp.ones((D,), dtype=jnp.float32), 'beta': jnp.zeros((D,), dtype=jnp.float32)}
    _L0_attn_all = _L0_attn_setup()
    _L0_attn_in = {k: v for k, v in _L0_attn_all.items() if k in ('w_qkv', 'w_out', 'b_out', 'gamma', 'beta')}
    del _L0_attn_all

    def _L0_xattn_setup():
        import jax, jax.numpy as jnp
        import numpy as np
        DIM = 128
        HEADS = 16
        DIM_HEAD = 64
        INNER = HEADS * DIM_HEAD
        EPS = 1e-05

        def layernorm(x, w, b):
            mu = jnp.mean(x, axis=-1, keepdims=True)
            var = jnp.mean(jnp.square(x - mu), axis=-1, keepdims=True)
            return (x - mu) * jax.lax.rsqrt(var + EPS) * w + b
        key = jax.random.key(seed)
        ks = jax.random.split(key, 9)
        b, n1, n2 = (4, 512, 32)
        x = jax.random.normal(ks[0], (b, n1, DIM), dtype=jnp.float32)
        latents = jax.random.normal(ks[1], (b, n2, DIM), dtype=jnp.float32)
        shift = jax.random.normal(ks[2], (b, HEADS), dtype=jnp.float32)
        scale = jax.random.normal(ks[3], (b, HEADS), dtype=jnp.float32)
        s = 1.0 / np.sqrt(DIM)
        Wq = jax.random.normal(ks[4], (DIM, INNER), dtype=jnp.float32) * s
        Wkv = jax.random.normal(ks[5], (DIM, 2 * INNER), dtype=jnp.float32) * s
        Wout = jax.random.normal(ks[6], (INNER, DIM), dtype=jnp.float32) * (1.0 / np.sqrt(INNER))
        ln1_w = jnp.ones((DIM,), jnp.float32)
        ln1_b = jnp.zeros((DIM,), jnp.float32)
        ln2_w = jnp.ones((DIM,), jnp.float32)
        ln2_b = jnp.zeros((DIM,), jnp.float32)
        return {'x': x, 'latents': latents, 'shift': shift, 'scale': scale, 'ln1_w': ln1_w, 'ln1_b': ln1_b, 'ln2_w': ln2_w, 'ln2_b': ln2_b, 'Wq': Wq, 'Wkv': Wkv, 'Wout': Wout}
    _L0_xattn_all = _L0_xattn_setup()
    _L0_xattn_in = {k: v for k, v in _L0_xattn_all.items() if k in ('ln1_w', 'ln1_b', 'ln2_w', 'ln2_b', 'Wq', 'Wkv', 'Wout')}
    del _L0_xattn_all

    def _L0_ffn_setup():
        import jax, jax.numpy as jnp
        import numpy as np
        K = 32
        key = jax.random.key(seed)
        ks = jax.random.split(key, 9)
        B, S, D, O, E = (8, 256, 128, 128, 16)

        def xavier(k_, shape):
            fan_in, fan_out = (shape[-2], shape[-1])
            lim = (6.0 / (fan_in + fan_out)) ** 0.5
            return jax.random.uniform(k_, shape, jnp.float32, -lim, lim)
        return {'x': jax.random.normal(ks[0], (B, S, D), jnp.float32), 'Wg': xavier(ks[1], (D, E)), 'bg': jnp.zeros((E,), jnp.float32), 'w1': xavier(ks[2], (E, D, O)), 'b1': xavier(ks[3], (E, 1)), 'w2': xavier(ks[4], (E, O, O)), 'b2': xavier(ks[5], (E, 1)), 'w3': xavier(ks[6], (E, O, O)), 'b3': xavier(ks[7], (E, 1))}
    _L0_ffn_all = _L0_ffn_setup()
    _L0_ffn_in = {k: v for k, v in _L0_ffn_all.items() if k in ('Wg', 'bg', 'w1', 'b1', 'w2', 'b2', 'w3', 'b3')}
    del _L0_ffn_all

    def _L1_attn_setup():
        import jax, jax.numpy as jnp
        import numpy as np
        from jax import lax
        DIM = 128
        HEADS = 16
        HEAD_DIM = DIM // HEADS
        BLOCK = 128
        DECAY = 0.9
        SPIKE_TH = 0.5
        K_WINNERS = 4
        HIDDEN = 4 * DIM
        EPS = 1e-05

        def _rmsnorm(x, w):
            norm = lax.rsqrt(jnp.mean(x * x, axis=-1, keepdims=True) + EPS)
            return w * x * norm

        def _spike_kwta(k):
            k = jnp.where(k > SPIKE_TH, k, 0.0)
            thr = lax.top_k(k, K_WINNERS)[0][..., -1:]
            return jnp.where(k >= thr, k, 0.0)

        def _mix(h, Wr, Wk, Wv, Wo):
            B, T, _ = h.shape
            N = T // BLOCK
            r = jax.nn.sigmoid((h @ Wr).reshape(B, T, HEADS, HEAD_DIM))
            k = _spike_kwta((h @ Wk).reshape(B, T, HEADS, HEAD_DIM))
            v = (h @ Wv).reshape(B, T, HEADS, HEAD_DIM)

            def chunks(a):
                return a.reshape(B, N, BLOCK, HEADS, HEAD_DIM).transpose(1, 0, 2, 3, 4)
            rc_all, kc_all, vc_all = (chunks(r), chunks(k), chunks(v))
            t_idx = jnp.arange(BLOCK, dtype=h.dtype)
            w_in = (DECAY ** (t_idx + 1.0))[None, :, None, None]
            w_out = (DECAY ** (BLOCK - 1.0 - t_idx))[None, :, None, None]
            lm = t_idx[:, None] - t_idx[None, :]
            mask = jnp.where(lm >= 0, DECAY ** lm, 0.0)
            w_L = DECAY ** BLOCK

            def step(S, inp):
                rc, kc, vc = inp
                inter = jnp.einsum('blhd,bhde->blhe', rc * w_in, S)
                A = jnp.einsum('blhd,bmhd->bhlm', rc, kc) * mask
                intra = jnp.einsum('bhlm,bmhe->blhe', A, vc)
                S_new = w_L * S + jnp.einsum('blhd,blhe->bhde', kc * w_out, vc)
                return (S_new, inter + intra)
            S0 = jnp.zeros((B, HEADS, HEAD_DIM, HEAD_DIM), h.dtype)
            _, y = lax.scan(step, S0, (rc_all, kc_all, vc_all))
            y = y.transpose(1, 0, 2, 3, 4).reshape(B, T, DIM)
            return y @ Wo
        key = jax.random.key(seed)
        ks = jax.random.split(key, 9)
        s = 0.02
        return {'x': jax.random.normal(ks[0], (2, 128, DIM), jnp.float32), 'norm1_w': jnp.ones((DIM,), jnp.float32), 'Wr': jax.random.normal(ks[1], (DIM, DIM), jnp.float32) * s, 'Wk': jax.random.normal(ks[2], (DIM, DIM), jnp.float32) * s + 0.5, 'Wv': jax.random.normal(ks[3], (DIM, DIM), jnp.float32) * s, 'Wo': jax.random.normal(ks[4], (DIM, DIM), jnp.float32) * s, 'norm2_w': jnp.ones((DIM,), jnp.float32), 'w1': jax.random.normal(ks[5], (DIM, HIDDEN), jnp.float32) * s, 'w2': jax.random.normal(ks[6], (DIM, HIDDEN), jnp.float32) * s, 'w3': jax.random.normal(ks[7], (HIDDEN, DIM), jnp.float32) * s}
    _L1_attn_all = _L1_attn_setup()
    _L1_attn_in = {k: v for k, v in _L1_attn_all.items() if k in ('norm1_w', 'Wr', 'Wk', 'Wv', 'Wo', 'norm2_w', 'w1', 'w2', 'w3')}
    del _L1_attn_all

    def _L1_xattn_setup():
        import jax, jax.numpy as jnp
        import numpy as np
        D_MODEL = 128
        NUM_HEADS = 16
        DEPTH = D_MODEL // NUM_HEADS

        def _split_heads(x, B):
            return x.reshape(B, -1, NUM_HEADS, DEPTH).transpose(0, 2, 1, 3)
        key = jax.random.key(seed)
        ks = jax.random.split(key, 11)
        B, S = (4, 256)
        scale = 1.0 / np.sqrt(D_MODEL)
        inp = {'query': jax.random.normal(ks[0], (B, S, D_MODEL), jnp.float32), 'key': jax.random.normal(ks[1], (B, S, D_MODEL), jnp.float32), 'value': jax.random.normal(ks[2], (B, S, D_MODEL), jnp.float32), 'wq_w': jax.random.normal(ks[3], (D_MODEL, D_MODEL), jnp.float32) * scale, 'wq_b': jnp.zeros((D_MODEL,), jnp.float32), 'wk_w': jax.random.normal(ks[4], (D_MODEL, D_MODEL), jnp.float32) * scale, 'wk_b': jnp.zeros((D_MODEL,), jnp.float32), 'wv_w': jax.random.normal(ks[5], (D_MODEL, D_MODEL), jnp.float32) * scale, 'wv_b': jnp.zeros((D_MODEL,), jnp.float32), 'dense_w': jax.random.normal(ks[6], (D_MODEL, D_MODEL), jnp.float32) * scale, 'dense_b': jnp.zeros((D_MODEL,), jnp.float32)}
        return inp
    _L1_xattn_all = _L1_xattn_setup()
    _L1_xattn_in = {k: v for k, v in _L1_xattn_all.items() if k in ('wq_w', 'wq_b', 'wk_w', 'wk_b', 'wv_w', 'wv_b', 'dense_w', 'dense_b')}
    del _L1_xattn_all

    def _L1_ffn_setup():
        import jax, jax.numpy as jnp
        import numpy as np
        EPS = 1e-05

        @jax.custom_vjp
        def ste_quantize(w):
            scale = jnp.maximum(jnp.mean(jnp.abs(w)), EPS)
            return jnp.clip(jnp.round(w / scale), -1.0, 1.0)

        def _ste_fwd(w):
            return (ste_quantize(w), None)

        def _ste_bwd(_, g):
            return (g,)
        ste_quantize.defvjp(_ste_fwd, _ste_bwd)
        key = jax.random.key(seed)
        k1, k2 = jax.random.split(key)
        x = jax.random.normal(k1, (8, 1024, 128), dtype=jnp.float32)
        weight = jax.random.normal(k2, (128, 128), dtype=jnp.float32) * 0.02
        return {'x': x, 'weight': weight}
    _L1_ffn_all = _L1_ffn_setup()
    _L1_ffn_in = {k: v for k, v in _L1_ffn_all.items() if k in ('weight',)}
    del _L1_ffn_all
    return {'x': x, 'ctx_1024': ctx_1024, 'fside_Bx16_0': fside_Bx16_0, 'L0_attn_w_qkv': _L0_attn_in['w_qkv'], 'L0_attn_w_out': _L0_attn_in['w_out'], 'L0_attn_b_out': _L0_attn_in['b_out'], 'L0_attn_gamma': _L0_attn_in['gamma'], 'L0_attn_beta': _L0_attn_in['beta'], 'L0_xattn_ln1_w': _L0_xattn_in['ln1_w'], 'L0_xattn_ln1_b': _L0_xattn_in['ln1_b'], 'L0_xattn_ln2_w': _L0_xattn_in['ln2_w'], 'L0_xattn_ln2_b': _L0_xattn_in['ln2_b'], 'L0_xattn_Wq': _L0_xattn_in['Wq'], 'L0_xattn_Wkv': _L0_xattn_in['Wkv'], 'L0_xattn_Wout': _L0_xattn_in['Wout'], 'L0_ffn_Wg': _L0_ffn_in['Wg'], 'L0_ffn_bg': _L0_ffn_in['bg'], 'L0_ffn_w1': _L0_ffn_in['w1'], 'L0_ffn_b1': _L0_ffn_in['b1'], 'L0_ffn_w2': _L0_ffn_in['w2'], 'L0_ffn_b2': _L0_ffn_in['b2'], 'L0_ffn_w3': _L0_ffn_in['w3'], 'L0_ffn_b3': _L0_ffn_in['b3'], 'L1_attn_norm1_w': _L1_attn_in['norm1_w'], 'L1_attn_Wr': _L1_attn_in['Wr'], 'L1_attn_Wk': _L1_attn_in['Wk'], 'L1_attn_Wv': _L1_attn_in['Wv'], 'L1_attn_Wo': _L1_attn_in['Wo'], 'L1_attn_norm2_w': _L1_attn_in['norm2_w'], 'L1_attn_w1': _L1_attn_in['w1'], 'L1_attn_w2': _L1_attn_in['w2'], 'L1_attn_w3': _L1_attn_in['w3'], 'L1_xattn_wq_w': _L1_xattn_in['wq_w'], 'L1_xattn_wq_b': _L1_xattn_in['wq_b'], 'L1_xattn_wk_w': _L1_xattn_in['wk_w'], 'L1_xattn_wk_b': _L1_xattn_in['wk_b'], 'L1_xattn_wv_w': _L1_xattn_in['wv_w'], 'L1_xattn_wv_b': _L1_xattn_in['wv_b'], 'L1_xattn_dense_w': _L1_xattn_in['dense_w'], 'L1_xattn_dense_b': _L1_xattn_in['dense_b'], 'L1_ffn_weight': _L1_ffn_in['weight']}

def reference(x, ctx_1024, fside_Bx16_0, L0_attn_w_qkv, L0_attn_w_out, L0_attn_b_out, L0_attn_gamma, L0_attn_beta, L0_xattn_ln1_w, L0_xattn_ln1_b, L0_xattn_ln2_w, L0_xattn_ln2_b, L0_xattn_Wq, L0_xattn_Wkv, L0_xattn_Wout, L0_ffn_Wg, L0_ffn_bg, L0_ffn_w1, L0_ffn_b1, L0_ffn_w2, L0_ffn_b2, L0_ffn_w3, L0_ffn_b3, L1_attn_norm1_w, L1_attn_Wr, L1_attn_Wk, L1_attn_Wv, L1_attn_Wo, L1_attn_norm2_w, L1_attn_w1, L1_attn_w2, L1_attn_w3, L1_xattn_wq_w, L1_xattn_wq_b, L1_xattn_wk_w, L1_xattn_wk_b, L1_xattn_wv_w, L1_xattn_wv_b, L1_xattn_dense_w, L1_xattn_dense_b, L1_ffn_weight):
    import jax
    import jax.numpy as jnp

    def _L0_attn_ref(x, w_qkv, w_out, b_out, gamma, beta):
        import jax, jax.numpy as jnp
        import numpy as np
        B, S, D, H = (4, 256, 128, 16)
        HD = D // H
        LN_EPS = 1e-05
        KERN_EPS = 1e-06

        def kernel_func(q, k):
            scores = jnp.einsum('bhqd,bhkd->bhqk', q, k) / jnp.sqrt(jnp.asarray(HD, q.dtype))
            w = jax.nn.relu(scores)
            return w / (jnp.sum(w, axis=-1, keepdims=True) + KERN_EPS)
        Bx, Sx, _ = x.shape
        qkv = (x @ w_qkv).reshape(Bx, Sx, H, 3 * HD)
        q, k, v = jnp.split(qkv, 3, axis=-1)
        q = q.transpose(0, 2, 1, 3)
        k = k.transpose(0, 2, 1, 3)
        v = v.transpose(0, 2, 1, 3)
        attn = kernel_func(q, k)
        out = jnp.einsum('bhqk,bhkd->bhqd', attn, v)
        out = out.transpose(0, 2, 1, 3).reshape(Bx, Sx, D)
        out = out @ w_out + b_out
        y = x + out
        mu = jnp.mean(y, axis=-1, keepdims=True)
        var = jnp.var(y, axis=-1, keepdims=True)
        return (y - mu) * jax.lax.rsqrt(var + LN_EPS) * gamma + beta

    def _L0_xattn_ref(x, latents, shift, scale, ln1_w, ln1_b, ln2_w, ln2_b, Wq, Wkv, Wout):
        import jax, jax.numpy as jnp
        import numpy as np
        DIM = 128
        HEADS = 16
        DIM_HEAD = 64
        INNER = HEADS * DIM_HEAD
        EPS = 1e-05

        def layernorm(x, w, b):
            mu = jnp.mean(x, axis=-1, keepdims=True)
            var = jnp.mean(jnp.square(x - mu), axis=-1, keepdims=True)
            return (x - mu) * jax.lax.rsqrt(var + EPS) * w + b
        b = x.shape[0]
        xn = layernorm(x, ln1_w, ln1_b)
        ln = layernorm(latents, ln2_w, ln2_b)
        q = ln @ Wq
        kv = xn @ Wkv
        k, v = jnp.split(kv, 2, axis=-1)
        q = q.reshape(b, -1, HEADS, DIM_HEAD)
        k = k.reshape(b, -1, HEADS, DIM_HEAD)
        v = v.reshape(b, -1, HEADS, DIM_HEAD)
        q = q * (1.0 + scale[:, None, :, None]) + shift[:, None, :, None]
        attn_scale = DIM_HEAD ** (-0.5)
        qk = jnp.einsum('bihd,bjhd->bhij', q.astype(jnp.float32), k.astype(jnp.float32)) * attn_scale
        attn = jax.nn.softmax(qk, axis=-1).astype(v.dtype)
        out = jnp.einsum('bhij,bjhd->bihd', attn, v)
        out = out.reshape(b, -1, INNER)
        return out @ Wout

    def _L0_ffn_ref(x, Wg, bg, w1, b1, w2, b2, w3, b3):
        import jax, jax.numpy as jnp
        import numpy as np
        K = 32
        B, S, D = x.shape
        E, _, O = w1.shape
        logits = jnp.einsum('bsd,de->bse', x, Wg) + bg
        probs = jax.nn.softmax(logits, axis=-2)
        pv = jnp.transpose(probs, (0, 2, 1))
        vals, idx = jax.lax.top_k(pv, K)
        bidx = jnp.arange(B)[:, None, None]
        tok = x[bidx, idx]
        b1b = b1[None, :, None, :]
        b2b = b2[None, :, None, :]
        b3b = b3[None, :, None, :]
        h = jax.nn.relu(jnp.einsum('bekd,edo->beko', tok, w1) + b1b)
        h = jax.nn.relu(jnp.einsum('bekd,edo->beko', h, w2) + b2b)
        h = jnp.einsum('bekd,edo->beko', h, w3) + b3b
        out = h * vals[..., None]
        outputs = jnp.zeros((B, S, O), x.dtype).at[bidx, idx].add(out)
        return outputs

    def _L1_attn_ref(x, norm1_w, Wr, Wk, Wv, Wo, norm2_w, w1, w2, w3):
        import jax, jax.numpy as jnp
        import numpy as np
        from jax import lax
        DIM = 128
        HEADS = 16
        HEAD_DIM = DIM // HEADS
        BLOCK = 128
        DECAY = 0.9
        SPIKE_TH = 0.5
        K_WINNERS = 4
        HIDDEN = 4 * DIM
        EPS = 1e-05

        def _rmsnorm(x, w):
            norm = lax.rsqrt(jnp.mean(x * x, axis=-1, keepdims=True) + EPS)
            return w * x * norm

        def _spike_kwta(k):
            k = jnp.where(k > SPIKE_TH, k, 0.0)
            thr = lax.top_k(k, K_WINNERS)[0][..., -1:]
            return jnp.where(k >= thr, k, 0.0)

        def _mix(h, Wr, Wk, Wv, Wo):
            B, T, _ = h.shape
            N = T // BLOCK
            r = jax.nn.sigmoid((h @ Wr).reshape(B, T, HEADS, HEAD_DIM))
            k = _spike_kwta((h @ Wk).reshape(B, T, HEADS, HEAD_DIM))
            v = (h @ Wv).reshape(B, T, HEADS, HEAD_DIM)

            def chunks(a):
                return a.reshape(B, N, BLOCK, HEADS, HEAD_DIM).transpose(1, 0, 2, 3, 4)
            rc_all, kc_all, vc_all = (chunks(r), chunks(k), chunks(v))
            t_idx = jnp.arange(BLOCK, dtype=h.dtype)
            w_in = (DECAY ** (t_idx + 1.0))[None, :, None, None]
            w_out = (DECAY ** (BLOCK - 1.0 - t_idx))[None, :, None, None]
            lm = t_idx[:, None] - t_idx[None, :]
            mask = jnp.where(lm >= 0, DECAY ** lm, 0.0)
            w_L = DECAY ** BLOCK

            def step(S, inp):
                rc, kc, vc = inp
                inter = jnp.einsum('blhd,bhde->blhe', rc * w_in, S)
                A = jnp.einsum('blhd,bmhd->bhlm', rc, kc) * mask
                intra = jnp.einsum('bhlm,bmhe->blhe', A, vc)
                S_new = w_L * S + jnp.einsum('blhd,blhe->bhde', kc * w_out, vc)
                return (S_new, inter + intra)
            S0 = jnp.zeros((B, HEADS, HEAD_DIM, HEAD_DIM), h.dtype)
            _, y = lax.scan(step, S0, (rc_all, kc_all, vc_all))
            y = y.transpose(1, 0, 2, 3, 4).reshape(B, T, DIM)
            return y @ Wo
        x = x + _mix(_rmsnorm(x, norm1_w), Wr, Wk, Wv, Wo)
        h = _rmsnorm(x, norm2_w)
        x = x + jax.nn.silu(h @ w1) * (h @ w2) @ w3
        return x

    def _L1_xattn_ref(query, key, value, wq_w, wq_b, wk_w, wk_b, wv_w, wv_b, dense_w, dense_b):
        import jax, jax.numpy as jnp
        import numpy as np
        D_MODEL = 128
        NUM_HEADS = 16
        DEPTH = D_MODEL // NUM_HEADS

        def _split_heads(x, B):
            return x.reshape(B, -1, NUM_HEADS, DEPTH).transpose(0, 2, 1, 3)
        B = query.shape[0]
        q = _split_heads(query @ wq_w.T + wq_b, B)
        k = _split_heads(key @ wk_w.T + wk_b, B)
        v = _split_heads(value @ wv_w.T + wv_b, B)
        scores = jnp.einsum('bhqd,bhkd->bhqk', q, k) / jnp.sqrt(jnp.float32(DEPTH)).astype(q.dtype)
        attn = jax.nn.softmax(scores, axis=-1)
        out = jnp.einsum('bhqk,bhkd->bhqd', attn, v)
        out = out.transpose(0, 2, 1, 3).reshape(B, -1, D_MODEL)
        return out @ dense_w.T + dense_b

    def _L1_ffn_ref(x, weight):
        import jax, jax.numpy as jnp
        import numpy as np
        EPS = 1e-05

        @jax.custom_vjp
        def ste_quantize(w):
            scale = jnp.maximum(jnp.mean(jnp.abs(w)), EPS)
            return jnp.clip(jnp.round(w / scale), -1.0, 1.0)

        def _ste_fwd(w):
            return (ste_quantize(w), None)

        def _ste_bwd(_, g):
            return (g,)
        ste_quantize.defvjp(_ste_fwd, _ste_bwd)
        w_ternary = ste_quantize(weight)
        scale = jnp.maximum(jnp.mean(jnp.abs(weight)), EPS)
        return jnp.einsum('bsi,oi->bso', x, w_ternary * scale)
    x = _layernorm(x + _L0_attn_ref(x, L0_attn_w_qkv, L0_attn_w_out, L0_attn_b_out, L0_attn_gamma, L0_attn_beta), axis=-1)
    x = _layernorm(x + _L0_xattn_ref(ctx_1024, x, fside_Bx16_0, fside_Bx16_0, L0_xattn_ln1_w, L0_xattn_ln1_b, L0_xattn_ln2_w, L0_xattn_ln2_b, L0_xattn_Wq, L0_xattn_Wkv, L0_xattn_Wout), axis=-1)
    x = _layernorm(x + _L0_ffn_ref(x, L0_ffn_Wg, L0_ffn_bg, L0_ffn_w1, L0_ffn_b1, L0_ffn_w2, L0_ffn_b2, L0_ffn_w3, L0_ffn_b3), axis=-1)
    x = _layernorm(x + _L1_attn_ref(x, L1_attn_norm1_w, L1_attn_Wr, L1_attn_Wk, L1_attn_Wv, L1_attn_Wo, L1_attn_norm2_w, L1_attn_w1, L1_attn_w2, L1_attn_w3), axis=-1)
    x = _layernorm(x + _L1_xattn_ref(x, ctx_1024, ctx_1024, L1_xattn_wq_w, L1_xattn_wq_b, L1_xattn_wk_w, L1_xattn_wk_b, L1_xattn_wv_w, L1_xattn_wv_b, L1_xattn_dense_w, L1_xattn_dense_b), axis=-1)
    x = _layernorm(x + _L1_ffn_ref(x, L1_ffn_weight), axis=-1)
    return x

_drawn_inputs = setup_inputs


def setup_inputs(seed=0):
    import zlib

    import numpy as np

    out = dict(_drawn_inputs(seed))
    spreads = {'L0_attn_b_out': (0.0, 0.1),
     'L0_attn_gamma': (1.0, 0.2),
     'L0_attn_beta': (0.0, 0.1),
     'L0_xattn_ln1_w': (1.0, 0.2),
     'L0_xattn_ln1_b': (0.0, 0.1),
     'L0_xattn_ln2_w': (1.0, 0.2),
     'L0_xattn_ln2_b': (0.0, 0.294),
     'L0_ffn_bg': (0.0, 0.8),
     'L1_attn_norm1_w': (1.0, 0.2),
     'L1_attn_norm2_w': (1.0, 0.6),
     'L1_xattn_wq_b': (0.0, 0.323),
     'L1_xattn_wk_b': (0.0, 0.8),
     'L1_xattn_wv_b': (0.0, 0.1),
     'L1_xattn_dense_b': (0.0, 0.1)}
    factors = {'L0_ffn_b1': 5.188,
     'L0_ffn_b2': 6.051,
     'L0_ffn_b3': 8.0,
     'L1_attn_Wr': 6.394,
     'L1_attn_Wk': 4.792,
     'L1_attn_w1': 8.0,
     'L1_attn_w2': 8.0,
     'L1_attn_w3': 8.0}
    for name, (base, spread) in spreads.items():
        noise = np.random.default_rng([zlib.crc32(name.encode()), seed]).standard_normal(out[name].shape)
        drawn = base * np.exp(spread * noise) if base else spread * noise
        out[name] = jnp.asarray(drawn.astype(out[name].dtype))
    for name, factor in factors.items():
        out[name] = (out[name] * factor).astype(out[name].dtype)
    return out
```

```python
from contextlib import ExitStack

import numpy as np

import concourse.bass as bass
from concourse import mybir

B, S, D = 16, 128, 128
C, CE = 77, 78
H, HD = 16, 8
XH, XD = 16, 64
XB = XH * XD // 128
E, TOPK = 16, 32
HID = 512
G4 = H // 4
DECAY = 0.9
LN_EPS, KERN_EPS = 1e-5, 1e-6
BANK = 512

SPLIT = [("qkv1", 3 * D), ("k2", XH * XD), ("v2", XH * XD), ("kv5", 2 * D), ("q2", XH * XD),
         ("gate", 128), ("exp1", E * D), ("rkv4", 3 * D), ("up4", 2 * HID), ("q5", D)]
WHOLE = [("out1", D), ("out2", XB * D), ("exp2", E * D), ("exp3", E * D), ("out4", D), ("down4", HID),
         ("out5", D), ("tern6", D)]
CONST = [("ident", 128), ("decay", 128), ("b_out", D), ("gamma", D), ("beta", D),
         ("ln1_w", D), ("ln1_b", D), ("ln2_w", D), ("ln2_b", D), ("rms1", D), ("rms2", D), ("bk5", D),
         ("bv5", D), ("bq5", D), ("bd5", D), ("b1", E), ("b2", E), ("b3", E), ("bg", 1)]


def offsets(parts):
    at, out = 0, {}
    for name, n in parts:
        out[name] = (at, at + n)
        at += n
    return out, at


SPLIT_AT, SPLIT_COLS = offsets(SPLIT)
WHOLE_AT, WHOLE_COLS = offsets(WHOLE)
CONST_AT, CONST_COLS = offsets(CONST)
STAGE = 1024
CHUNKS = [(a, min(a + STAGE, SPLIT_COLS)) for a in range(0, SPLIT_COLS, STAGE)]

LINKS = {"dve_first": 20, "dve_second": 57, "pool_first": 10, "pool_second": 10}

STEPS = 11
FIRST_COST = [1.5, 2, 2, 1, 2.5, 3.5, 3, 5, 4, 3, 4, 2, 6, 4, 3.5, 3.5]
SECOND_COST = [1.5, 5, 1.5] + [1.5] * STEPS + [4, 2, 4, 1.5, 2.5, 2, 1.5, 3.5, 2, 4, 3, 2, 1.5, 1, 2.5, 2, 3, 2, 1.5, 4, 1, 4]


def merge_order():
    marks = []
    for which, costs in (("second", SECOND_COST), ("first", FIRST_COST)):
        total, at = sum(costs), 0
        for c in costs:
            at += c
            marks.append((at / total, which))
    return [which for _, which in sorted(marks, key=lambda m: m[0])]


ORDER = merge_order()


def together(second, first):
    halves = {"second": second, "first": first}
    for which in ORDER:
        next(halves[which])
    for half in halves.values():
        for _ in half:
            raise AssertionError("a phase is missing in the costs")


def alone(half):
    for _ in half:
        pass


def decoder(nc, x, ctx, fside, w_split, w_whole, const, picker, out):
    F, R = mybir.dt.float32, mybir.dt.float32r
    ALU, ACT, AX = mybir.AluOpType, mybir.ActivationFunctionType, mybir.AxisListType
    held = ExitStack()
    with held:
        def sb(name, cols, dt=F, rows=128):
            return held.enter_context(nc.sbuf_tensor(name, [rows, cols], dt))

        sems = {}

        def sem(name):
            if name not in sems:
                sems[name] = held.enter_context(nc.semaphore(name))
            return sems[name]

        w_hi, w_lo = sb("w_hi", SPLIT_COLS, R), sb("w_lo", SPLIT_COLS, R)
        whole = sb("whole", WHOLE_COLS)
        cst = sb("cst", CONST_COLS)
        ident_r = sb("ident_r", 128, R)
        pick_r = sb("pick_r", XH * CE, R)
        half_exp = sb("half_exp", 1)
        ones = sb("ones", 128)
        t_abs, t_scale, t_half, t_neg = sb("t_abs", 1), sb("t_scale", 1), sb("t_half", 1), sb("t_neg", 1)
        t_low = sb("t_low", D)
        ps = [held.enter_context(nc.psum_tensor(f"ps{s}", [128, 4 * BANK], F)) for s in range(2)]

        def slots(name, cols, dt=F, rows=128):
            return [sb(f"{name}{s}", cols, dt, rows) for s in range(2)]

        xin, cin, fs, fs1 = slots("xin", D), slots("cin", D, rows=CE), slots("fs", XB), slots("fs1", 2 * XB)
        xs, hs = slots("xs", D), slots("hs", D)
        xbias, xres = slots("xbias", D), slots("xres", D)
        zz, yy = slots("zz", D), slots("yy", D)
        res = slots("res", D)
        cn, kb = slots("cn", D, rows=CE), slots("kb", D, rows=CE)
        xp, xt = slots("xp", 2 * D, R), slots("xt", 2 * D, R)
        cp = slots("cp", 4 * D, R, rows=CE)
        ct = slots("ct", 4 * CE, R)
        q4, k4 = slots("q4", 4 * D, R), slots("k4", 4 * D, R)
        qt, kt = slots("qt", 4 * D, R), slots("kt", 4 * D, R)
        k45, kt5 = cp, slots("kt5", 4 * CE, R)
        v9, v95 = slots("v9", H * 9), slots("v95", H * 9, rows=CE)
        v65 = slots("v65", XH * 65, rows=CE)
        qt2, kt2 = slots("qt2", XB * S), slots("kt2", XB * CE)
        prob = slots("prob", H * S)
        big = slots("big", 2 * XH * XD)
        stage = [t[:, 0:STAGE] for t in big]
        pick = prob[0][:, 0:XH * CE]
        oo, ot = slots("oo", D), slots("ot", D)
        den, rec = slots("den", H), slots("rec", H)
        neg_max = slots("neg_max", H)
        nm, nmt = slots("nm", 128, R), slots("nmt", S, R)
        stats, mv, veps, rstd = slots("stats", 6), slots("mv", 2 * 11), slots("veps", 1), slots("rstd", 11)
        junk, gb = slots("junk", D), slots("gb", 1)
        lg, prb, left = slots("lg", S, rows=E), slots("prb", S, rows=E), slots("left", S, rows=E)
        gate, top8 = slots("gate", S, rows=E), slots("top8", 8, rows=E)
        esum = slots("esum", 3, rows=E)
        gt = slots("gt", E)
        acc = slots("acc", 2 * D)

        LN1, LN2 = ["ctx", "y1", "z1", "q2", "z2"], ["z3", "r1", "r2", "z4", "z5", "z6"]
        LNS = {n: i for i, n in enumerate(LN1 + LN2)}

        def ln_sem(name, what):
            return sem(f"{what}_first" if name in LN1 else f"{what}_second")

        def ln_count(name, b):
            order = LN1 if name in LN1 else LN2
            return b * len(order) + order.index(name) + 1

        ROWS1, ROWS2 = ["x1", "h2"], ["x3", "h4", "h5", "x5"]

        def rows_sem(name, what):
            return sem(f"rows_{what}_first" if name in ROWS1 else f"rows_{what}_second")

        def rows_count(name, b):
            order = ROWS1 if name in ROWS1 else ROWS2
            return b * len(order) + order.index(name) + 1

        def split_w(name, part, a=0, b=None):
            at = SPLIT_AT[name]
            return (w_hi, w_lo)[part][:, at[0] + a:at[0] + b if b else at[1]]

        def whole_w(name, a=0, b=None):
            at = WHOLE_AT[name]
            return whole[:, at[0] + a:at[0] + b if b else at[1]]

        def row(name, rows=128):
            at = CONST_AT[name]
            return cst[0:rows, at[0]:at[1]]

        def heads(t, n=H, rows=128):
            return t[0:rows, :].rearrange("p (h c) -> p h c", h=n)

        def loads(b, s):
            return b * 8 + (16 - 8 * s)

        block = held.enter_context(nc.Block())

        def wait_apart(eng, semaphore, value):
            if type(value) is not int:
                value = eng.to_reg(value)
                eng.wait_ge(sem("const_loaded"), 16)
            eng.wait_ge(semaphore, value)

        def whole_run(eng, first, second):
            alone(first(0, 1, 0))
            with eng.Fori(0, B // 2 - 1) as i:
                b = eng.snap(i * 2)
                n1 = eng.snap(b + 1)
                n2 = eng.snap(b + 2)
                n3 = eng.snap(b + 3)
                together(second(b, n1, 0), first(n1, n2, 1))
                together(second(n1, n2, 1), first(n2, n3, 0))
            together(second(B - 2, B - 1, 0), first(B - 1, B, 1))
            alone(second(B - 1, B, 1))

        @block.sync
        def _(sp):
            def load(b, s):
                sp.dma_start(xin[s][:, :], x[bass.ds(b, 1), :, :].rearrange("b p n -> (b p) n")).then_inc(sem(f"x_loaded{s}"), 16)
                sp.dma_start(cin[s][0:C, :], ctx[bass.ds(b, 1), :, :].rearrange("b p n -> (b p) n")).then_inc(sem(f"c_loaded{s}"), 16)
                sp.dma_start(fs[s][:, :], fside[bass.ds(b, 1), :, :].rearrange("b p n -> (b p) n")).then_inc(sem(f"f_loaded{s}"), 16)

            def store(b, s):
                sp.dma_start(out[bass.ds(b, 1), :, :].rearrange("b p n -> (b p) n"), res[s][:, :]).then_inc(sem("stored"), 16)

            sp.wait_ge(sem("zeroed"), 1)
            load(0, 0)
            sp.dma_start(cst[:, :], const).then_inc(sem("const_loaded"), 16)
            sp.dma_start(pick, picker).then_inc(sem("pick_loaded"), 16)
            for k, (a, e) in enumerate(CHUNKS):
                if k >= 2:
                    sp.wait_ge(sem("w_split"), k - 1)
                sp.dma_start(stage[k % 2][:, 0:e - a], w_split[:, a:e]).then_inc(sem(f"w_staged{k % 2}"), 16)
                if k == 0:
                    load(1, 1)
            sp.dma_start(whole[:, :], w_whole).then_inc(sem("whole_loaded"), 16)

            sp.wait_ge(sem("x_used"), 1)
            sp.wait_ge(sem("cn_split"), 1)
            load(2, 0)
            with sp.Fori(0, B // 2 - 2) as i:
                b = sp.snap(i * 2)
                n = [sp.snap(b + k) for k in range(1, 5)]
                free = [sp.snap(b * 16 + 16 * (k + 1)) for k in range(2)]
                for s in range(2):
                    wait_apart(sp, sem("out_ready"), n[s])
                    store(b if s == 0 else n[0], s)
                    wait_apart(sp, sem("stored"), free[s])
                    sp.wait_ge(sem("x_used"), n[s + 1])
                    sp.wait_ge(sem("cn_split"), n[s + 1])
                    load(n[s + 2], 1 - s)
            b = B - 4
            sp.wait_ge(sem("out_ready"), b + 1)
            store(b, 0)
            sp.wait_ge(sem("stored"), 16 * (b + 1))
            sp.wait_ge(sem("x_used"), b + 2)
            sp.wait_ge(sem("cn_split"), b + 2)
            load(b + 3, 1)
            for k in range(1, 4):
                sp.wait_ge(sem("out_ready"), b + k + 1)
                store(b + k, k % 2)
                sp.wait_ge(sem("stored"), 16 * (b + k + 1))

        @block.gpsimd
        def _(pool):
            for s in range(2):
                pool.memset(cin[s][:, :], 0.0).then_inc(sem("z0"), 1)
            pool.wait_ge(sem("z0"), 2)
            pool.memset(half_exp[:, :], -0.5).then_inc(sem("zeroed"), 1)
            for s in range(2):
                pool.memset(v9[s][:, :], 1.0)
                pool.memset(v95[s][:, :], 1.0)
                pool.memset(v65[s][:, :], 1.0)
                pool.memset(cn[s][:, :], 0.0)
            pool.memset(ones[:, :], 1.0).then_inc(sem("ones_set"), 1)
            pool.wait_ge(sem("ones_set"), 1)
            pool.wait_ge(sem("const_loaded"), 16)

            def link_on(name, b):
                count, total = [0], LINKS[name]
                base = 0 if type(b) is int and b == 0 else (b * total if type(b) is int else pool.snap(b * total))

                def link(ins):
                    count[0] += 1
                    ins.then_inc(sem(name), 1)
                    wait_apart(pool, sem(name), base + count[0])
                return link, count

            def inv_sqrt(link, b, s, name, scale=1.0, rows=128):
                k = LNS[name]
                wait_apart(pool, ln_sem(name, "var"), ln_count(name, b))
                link(pool.tensor_scalar(veps[s][0:rows, :], mv[s][0:rows, 2 * k + 1:2 * k + 2], scale, LN_EPS, ALU.mult, ALU.add))
                pool.tensor_tensor(out=rstd[s][0:rows, k:k + 1], in0=veps[s][0:rows, :], in1=half_exp[0:rows, :], op=ALU.pow).then_inc(ln_sem(name, "rstd"), 1)

            def split(link, src, hi, lo, done):
                link(pool.tensor_copy(hi, src))
                pool.tensor_tensor(out=lo, in0=src, in1=hi.bitcast(F), op=ALU.subtract).then_inc(done, 1)

            def first(b, n, s):
                link, count = link_on("pool_first", b)
                wait_apart(pool, sem(f"x_loaded{s}"), loads(b, s))
                split(link, xin[s][:, :], xp[s][:, 0:D], xp[s][:, D:2 * D], rows_sem("x1", "split"))
                pool.tensor_tensor(out=xbias[s][:, :], in0=xin[s][:, :], in1=row("b_out"), op=ALU.add).then_inc(sem("xbias1"), 1)
                pool.tensor_tensor(out=xres[s][:, :], in0=xin[s][:, :], in1=row("beta"), op=ALU.add).then_inc(sem("x_used"), 1)
                wait_apart(pool, sem(f"c_loaded{s}"), loads(b, s))
                inv_sqrt(link, b, s, "ctx", rows=C)
                split(link, cin[s][:, :], cp[s][:, 2 * D:3 * D], cp[s][:, 3 * D:4 * D], sem("c_used"))
                wait_apart(pool, sem(f"f_loaded{s}"), loads(b, s))
                pool.tensor_copy(fs1[s][:, XB:2 * XB], fs[s][:, :])
                pool.tensor_scalar(fs1[s][:, 0:XB], fs[s][:, :], 1.0, None, ALU.add).then_inc(sem("scale_ready"), 1)
                yield
                wait_apart(pool, sem("cn_ready"), n)
                split(link, cn[s][:, :], cp[s][:, 0:D], cp[s][:, D:2 * D], sem("cn_split"))
                yield
                for _ in range(4):
                    yield
                wait_apart(pool, sem("kb_ready"), n)
                kv = heads(kb[s], rows=CE).unsqueeze(2).broadcast_to([CE, H, 2, HD])
                k45v = k45[s][:, :].rearrange("p (h a c) -> p h a c", h=H, a=4)
                link(pool.tensor_copy(k45v[:, :, 0:2, :], kv))
                pool.tensor_tensor(out=k45v[:, :, 2:4, :], in0=kv, in1=k45v[:, :, 0:2, :].bitcast(F), op=ALU.subtract).then_inc(sem("k5_split"), 1)
                yield
                inv_sqrt(link, b, s, "y1")
                inv_sqrt(link, b, s, "z1")
                yield
                inv_sqrt(link, b, s, "q2")
                wait_apart(pool, sem("h2_ready"), n)
                split(link, hs[s][:, :], xp[s][:, 0:D], xp[s][:, D:2 * D], rows_sem("h2", "split"))
                yield
                for _ in range(6):
                    yield
                inv_sqrt(link, b, s, "z2")
                assert count[0] == LINKS["pool_first"], ("pool_first", count)
                yield

            def second(b, n, s):
                link, count = link_on("pool_second", b)
                wait_apart(pool, sem("x2_ready"), n)
                split(link, xs[s][:, :], xp[s][:, 0:D], xp[s][:, D:2 * D], rows_sem("x3", "split"))
                yield
                for _ in range(2 + STEPS):
                    yield
                inv_sqrt(link, b, s, "z3")
                inv_sqrt(link, b, s, "r1", 1.0 / D)
                wait_apart(pool, sem("h4_ready"), n)
                split(link, hs[s][:, :], xp[s][:, 0:D], xp[s][:, D:2 * D], rows_sem("h4", "split"))
                yield
                yield
                yield
                yield
                pool.wait_ge(sem("a4_moved"), n)
                p4 = prob[s][:, 0:2 * BANK].rearrange("p (g q) -> p g q", q=S)
                pool.tensor_tensor(out=p4, in0=p4, in1=row("decay").unsqueeze(1).broadcast_to([128, 8, S]), op=ALU.mult).then_inc(sem("a4_decayed"), 1)
                yield
                yield
                yield
                inv_sqrt(link, b, s, "r2", 1.0 / D)
                wait_apart(pool, sem("h5_ready"), n)
                split(link, hs[s][:, :], xp[s][:, 0:D], xp[s][:, D:2 * D], rows_sem("h5", "split"))
                pool.tensor_tensor(out=xres[s][:, :], in0=xs[s][:, :], in1=yy[s][:, :], op=ALU.add).then_inc(sem("xx4"), 1)
                yield
                wait_apart(pool, sem("exp_u"), n)
                hid = big[s][:, 0:HID]
                pool.tensor_scalar(hid, hid, 1.0, None, ALU.add).then_inc(sem("one_plus_u"), 1)
                yield
                inv_sqrt(link, b, s, "z4")
                yield
                wait_apart(pool, sem("x4_ready"), n)
                split(link, xs[s][:, :], xp[s][:, 0:D], xp[s][:, D:2 * D], rows_sem("x5", "split"))
                pool.tensor_tensor(out=xbias[s][:, :], in0=xs[s][:, :], in1=row("bd5"), op=ALU.add).then_inc(sem("xbias5"), 1)
                yield
                for _ in range(7):
                    yield
                yield
                inv_sqrt(link, b, s, "z5")
                yield
                yield
                inv_sqrt(link, b, s, "z6")
                assert count[0] == LINKS["pool_second"], ("pool_second", count)
                yield

            whole_run(pool, first, second)

        @block.scalar
        def _(act):
            act.wait_ge(sem("const_loaded"), 16)
            act.activation(ident_r[:, :], row("ident"), ACT.Copy).then_inc(sem("ident_ready"), 1)
            act.wait_ge(sem("pick_loaded"), 16)
            act.activation(pick_r[:, :], pick, ACT.Copy).then_inc(sem("ident_ready"), 1)
            for k, (a, e) in enumerate(CHUNKS):
                act.wait_ge(sem(f"w_staged{k % 2}"), 16 * (k // 2 + 1))
                act.activation(w_hi[:, a:e], stage[k % 2][:, 0:e - a], ACT.Copy).then_inc(sem("w_rounded"), 1)

            def move(dst, src, wait, n, signal, func=ACT.Copy, **kw):
                if wait:
                    act.wait_ge(sem(wait), n)
                act.activation(dst, src, func, **kw).then_inc(sem(signal), 1)

            def rows_back(p, b, s, name):
                act.wait_ge(rows_sem(name, "turned"), rows_count(name, b))
                act.activation(xt[s][:, :], p[:, 0:2 * D], ACT.Copy).then_inc(rows_sem(name, "back"), 1)

            def first(b, n, s):
                p = ps[s]
                rows_back(p, b, s, "x1")
                yield
                act.wait_ge(sem("qkv1_ready"), n)
                qk = p[:, BANK:BANK + 2 * D].rearrange("p (t h c) -> p t h c", t=2, h=H)
                q4v = q4[s][:, :].rearrange("p (h a c) -> p h a c", h=H, a=4)
                k4v = k4[s][:, :].rearrange("p (h a c) -> p h a c", h=H, a=4)
                act.activation(q4v[:, :, 0::2, :], qk[:, 0].unsqueeze(2).broadcast_to([128, H, 2, HD]), ACT.Copy)
                act.activation(k4v[:, :, 0:2, :], qk[:, 1].unsqueeze(2).broadcast_to([128, H, 2, HD]), ACT.Copy)
                act.activation(heads(v9[s])[:, :, 0:HD], heads(p[:, BANK + 2 * D:BANK + 3 * D]), ACT.Copy).then_inc(sem("v1_ready"), 1)
                yield
                move(qt[s][:, :], p[:, 2 * BANK:3 * BANK], "q1_turned", n, "q1t_ready")
                yield
                yield
                move(prob[s][:, 0:2 * BANK], p[:, 0:2 * BANK], "a1_ready", n, "p1_act", ACT.Relu, scale=HD ** -0.5)
                yield
                act.wait_ge(sem("k2_ready"), n)
                act.activation(kt2[s][:, :].rearrange("p (a m) -> p a m", a=2),
                               p[:, 2 * BANK:4 * BANK].rearrange("p (a m) -> p a m", a=2)[:, :, 0:4 * CE], ACT.Copy).then_inc(sem("k2t_ready"), 1)
                yield
                move(ot[s][:, :], p[:, 0:D], "o1_turned", n, "o1t_ready")
                act.wait_ge(sem("v2_ready"), n)
                act.activation(heads(v65[s], XH, CE)[:, 0:8, 0:XD], heads(p[:, 2 * BANK:3 * BANK], 8, CE), ACT.Copy).then_inc(sem("v2_act"), 1)
                yield
                move(kt5[s][:, :], p[:, BANK:BANK + 4 * CE], "k5_turned", n, "k5t_ready")
                yield
                rows_back(p, b, s, "h2")
                yield
                act.wait_ge(sem("scale_ready"), n)
                act.wait_ge(sem("q2_ready"), n)
                for k in range(4):
                    act.activation(qt2[s][:, k * S:(k + 1) * S], p[:, k * S:(k + 1) * S], ACT.Identity,
                                   scale=fs1[s][:, k:k + 1], bias=fs1[s][:, XB + k:XB + k + 1]).then_inc(sem("q2t_act"), 1)
                yield
                yield
                move(nmt[s][:, :], p[:, 0:S], "m2_turned", n, "m2t_ready")
                yield
                move(prob[s][0:C, 0:2 * BANK], p[0:C, 0:2 * BANK], "s2_first", n, "p2_first", ACT.Exp, scale=XD ** -0.5)
                move(prob[s][0:C, 2 * BANK:4 * BANK], p[0:C, 2 * BANK:4 * BANK], "s2_last", n, "p2_last", ACT.Exp, scale=XD ** -0.5)
                yield
                yield
                move(big[s][:, 1024:1536], p[:, 0:BANK], "o2_turned", n, "o2t_act")
                yield
                yield

            def second(b, n, s):
                p = ps[s]
                rows_back(p, b, s, "x3")
                yield
                act.wait_ge(sem("lg_max"), n)
                act.activation(prb[s][:, :], lg[s][:, :], ACT.Exp, bias=esum[s][:, 0:1], accum_out=esum[s][:, 1:2]).then_inc(sem("lg_exp"), 1)
                yield
                yield
                b8 = b * 8
                for e2 in range(STEPS):
                    if e2 < 8:
                        act.wait_ge(sem("e1_ready"), b8 + e2 + 1)
                        for e in (2 * e2, 2 * e2 + 1):
                            r = act.activation(prob[s][:, e * S:(e + 1) * S], p[:, e2 % 2 * 3 * BANK + e % 2 * S:e2 % 2 * 3 * BANK + (e % 2 + 1) * S], ACT.Relu, bias=row("b1")[:, e:e + 1])
                        r.then_inc(sem("e1_relu"), 1)
                    if 1 <= e2 < 9:
                        act.wait_ge(sem("e2_ready"), b8 + e2)
                        for e in (2 * e2 - 2, 2 * e2 - 1):
                            r = act.activation(big[s][:, e * S:(e + 1) * S], p[:, BANK + e % 2 * S:BANK + (e % 2 + 1) * S], ACT.Relu, bias=row("b2")[:, e:e + 1])
                        r.then_inc(sem("e2_relu"), 1)
                    yield
                rows_back(p, b, s, "h4")
                yield
                act.wait_ge(sem("rkv4_ready"), n)
                act.activation(oo[s][:, :], p[:, BANK:BANK + D], ACT.Exp, scale=-1.0).then_inc(sem("exp_r"), 1)
                act.activation(junk[s][:, :], p[:, BANK + D:BANK + 2 * D], ACT.Copy).then_inc(sem("k4_moved"), 1)
                act.activation(heads(v9[s])[:, :, 0:HD], heads(p[:, BANK + 2 * D:BANK + 3 * D]), ACT.Copy).then_inc(sem("v4_ready"), 1)
                yield
                yield
                move(qt[s][:, :], p[:, 2 * BANK:3 * BANK], "r4_turned", n, "r4t_ready")
                yield
                move(prob[s][:, 0:2 * BANK], p[:, 0:2 * BANK], "a4_ready", n, "a4_moved")
                yield
                move(oo[s][:, :], p[:, 0:D], "y4_ready", n, "y4_moved")
                yield
                move(ot[s][:, :], p[:, 0:D], "y4_turned", n, "y4t_ready")
                yield
                rows_back(p, b, s, "h5")
                yield
                move(big[s][:, 0:HID], p[:, 0:HID], "up4_ready", n, "exp_u", ACT.Exp, scale=-1.0)
                yield
                yield
                rows_back(p, b, s, "x5")
                yield
                act.wait_ge(sem("q5_ready"), n)
                yield
                move(qt[s][:, :], p[:, 2 * BANK:3 * BANK], "q5_turned", n, "q5t_ready")
                yield
                yield
                move(nmt[s][:, :], p[:, 0:S], "m5_turned", n, "m5t_ready")
                yield
                act.wait_ge(sem("s5t_ready"), n)
                for k in range(2):
                    act.activation(prob[s][0:C, 2 * k * BANK:2 * (k + 1) * BANK], p[0:C, 2 * k * BANK:2 * (k + 1) * BANK],
                                   ACT.Exp, scale=HD ** -0.5).then_inc(sem("p5_ready"), 1)
                yield
                yield
                move(ot[s][:, :], p[:, 0:D], "o5_turned", n, "o5t_ready")
                yield
                yield
                move(ot[s][:, :], p[:, 0:D], "x6_turned", n, "x6t_ready")
                yield
                yield
                yield

            whole_run(act, first, second)

        @block.vector
        def _(dve):
            v = nc.vector

            for k, (a, e) in enumerate(CHUNKS):
                dve.wait_ge(sem("w_rounded"), k + 1)
                v.tensor_tensor(w_lo[:, a:e], stage[k % 2][:, 0:e - a], w_hi[:, a:e].bitcast(F), ALU.subtract).then_inc(sem("w_split"), 1)
            dve.wait_ge(sem("ones_set"), 1)
            dve.wait_ge(sem("const_loaded"), 16)

            def ternary():
                tern = whole_w("tern6")
                v.tensor_reduce(t_abs[:, :], tern, AX.X, ALU.add, apply_absolute_value=True).then_inc(sem("t_abs"), 1)
                dve.wait_ge(sem("t_sum"), 1)
                v.tensor_scalar(t_scale[:, :], ps[1][:, 0:1], 1.0 / (D * D), LN_EPS, ALU.mult, ALU.max).then_inc(sem("t_link"), 1)
                dve.wait_ge(sem("t_link"), 1)
                v.tensor_scalar(t_half[:, :], t_scale[:, :], 0.5, None, ALU.mult)
                v.tensor_scalar(t_neg[:, :], t_scale[:, :], -0.5, None, ALU.mult).then_inc(sem("t_link"), 1)
                dve.wait_ge(sem("t_link"), 2)
                v.tensor_scalar(t_low[:, :], tern, t_neg[:, :], None, ALU.is_lt).then_inc(sem("t_link"), 1)
                dve.wait_ge(sem("t_link"), 3)
                v.scalar_tensor_tensor(tern, tern, t_half[:, :], t_low[:, :], ALU.is_gt, ALU.subtract).then_inc(sem("t_link"), 1)
                dve.wait_ge(sem("t_link"), 4)
                v.tensor_scalar(tern, tern, t_scale[:, :], None, ALU.mult).then_inc(sem("tern_ready"), 1)

            def link_on(name, b):
                count, total = [0], LINKS[name]
                base = 0 if type(b) is int and b == 0 else (b * total if type(b) is int else dve.snap(b * total))

                def link(ins, apart=False):
                    count[0] += 1
                    ins.then_inc(sem(name), 1)
                    if apart:
                        wait_apart(dve, sem(name), base + count[0])
                    else:
                        dve.wait_ge(sem(name), base + count[0])
                return link, count

            def var(link, z, s, name, rows=128):
                k = LNS[name]
                link(v.bn_stats(stats[s][0:rows, :], z), apart=True)
                v.bn_aggr(mv[s][0:rows, 2 * k:2 * k + 2], stats[s][0:rows, :]).then_inc(ln_sem(name, "var"), 1)

            def norm(out_, z, b, s, name, rows=128):
                k = LNS[name]
                dve.wait_ge(ln_sem(name, "rstd"), ln_count(name, b))
                return v.tensor_scalar(out_, z, mv[s][0:rows, 2 * k:2 * k + 1], rstd[s][0:rows, k:k + 1], ALU.subtract, ALU.mult)

            def weighted(link, p, s, hd, signal):
                link(v.reciprocal(rec[s][:, :], den[s][:, :]))
                v.tensor_tensor(heads(oo[s]), p[:, :, 0:hd], rec[s][:, :].unsqueeze(2).broadcast_to([128, H, hd]), ALU.mult).then_inc(sem(signal), 1)

            def split_max(link, s):
                parts = nm[s][:, :].rearrange("p (r a h) -> p r a h", r=4, a=2)
                m = neg_max[s][:, :].unsqueeze(1).broadcast_to([128, 4, H])
                link(v.tensor_copy(parts[:, :, 0, :], m))
                return v.tensor_tensor(parts[:, :, 1, :], m, parts[:, :, 0, :].bitcast(F), ALU.subtract)

            def dups(t):
                return t.unsqueeze(2).broadcast_to([t.shape[0], H, 2, HD])

            def first(b, n, s):
                p = ps[s]
                link, count = link_on("dve_first", b)
                dve.wait_ge(sem(f"c_loaded{s}"), loads(b, s))
                var(link, cin[s][0:C, :], s, "ctx", C)
                link(norm(cn[s][0:C, :], cin[s][0:C, :], b, s, "ctx", C))
                link(v.tensor_tensor(cn[s][0:C, :], cn[s][0:C, :], row("ln1_w", C), ALU.mult))
                v.tensor_tensor(cn[s][0:C, :], cn[s][0:C, :], row("ln1_b", C), ALU.add).then_inc(sem("cn_ready"), 1)
                yield
                dve.wait_ge(sem("v1_ready"), n)
                qk = p[:, BANK:BANK + 2 * D].rearrange("p (t h c) -> p t h c", t=2, h=H)
                q4v = q4[s][:, :].rearrange("p (h a c) -> p h a c", h=H, a=4)
                k4v = k4[s][:, :].rearrange("p (h a c) -> p h a c", h=H, a=4)
                v.tensor_tensor(q4v[:, :, 1::2, :], dups(qk[:, 0]), q4v[:, :, 0::2, :].bitcast(F), ALU.subtract)
                v.tensor_tensor(k4v[:, :, 2:4, :], dups(qk[:, 1]), k4v[:, :, 0:2, :].bitcast(F), ALU.subtract).then_inc(sem("qk1_split"), 1)
                yield
                dve.wait_ge(sem("k1_turned"), n)
                v.tensor_copy(kt[s][:, :], p[:, 3 * BANK:4 * BANK]).then_inc(sem("k1t_ready"), 1)
                yield
                dve.wait_ge(sem("c_turned"), n)
                v.tensor_copy(ct[s][:, :], p[:, 0:4 * CE]).then_inc(sem("ct_ready"), 1)
                yield
                dve.wait_ge(sem("a1_ready"), n)
                v.tensor_scalar(prob[s][:, 2 * BANK:4 * BANK], p[:, 2 * BANK:4 * BANK], HD ** -0.5, 0.0, ALU.mult, ALU.max).then_inc(sem("p1_dve"), 1)
                yield
                dve.wait_ge(sem("o1_ready"), n)
                o = heads(p[:, 0:H * 9])
                link(v.tensor_scalar(den[s][:, :], o[:, :, HD], KERN_EPS, None, ALU.add))
                weighted(link, o, s, HD, "o1_normed")
                dve.wait_ge(sem("kv5_ready"), n)
                v.tensor_tensor(kb[s][:, :], p[0:CE, BANK:BANK + D], row("bk5", CE), ALU.add).then_inc(sem("kb_ready"), 1)
                v.tensor_tensor(heads(v95[s], rows=CE)[:, :, 0:HD], heads(p[:, BANK + D:BANK + 2 * D], rows=CE),
                                row("bv5", CE).rearrange("p (h c) -> p h c", h=H), ALU.add).then_inc(sem("v5_ready"), 1)
                yield
                dve.wait_ge(sem("v2_ready"), n)
                v.tensor_copy(heads(v65[s], XH, CE)[:, 8:16, 0:XD], heads(p[:, 3 * BANK:4 * BANK], 8, CE)).then_inc(sem("v2_dve"), 1)
                yield
                dve.wait_ge(sem("y1_ready"), n)
                dve.wait_ge(sem("x_used"), n)
                link(v.tensor_tensor(yy[s][:, :], p[:, 0:D], xbias[s][:, :], ALU.add))
                var(link, yy[s][:, :], s, "y1")
                link(norm(yy[s][:, :], yy[s][:, :], b, s, "y1"))
                link(v.tensor_tensor(yy[s][:, :], yy[s][:, :], row("gamma"), ALU.mult))
                link(v.tensor_tensor(zz[s][:, :], yy[s][:, :], xres[s][:, :], ALU.add))
                var(link, zz[s][:, :], s, "z1")
                link(norm(xs[s][:, :], zz[s][:, :], b, s, "z1"))
                yield
                var(link, xs[s][:, :], s, "q2")
                link(norm(hs[s][:, :], xs[s][:, :], b, s, "q2"))
                link(v.tensor_tensor(hs[s][:, :], hs[s][:, :], row("ln2_w"), ALU.mult))
                v.tensor_tensor(hs[s][:, :], hs[s][:, :], row("ln2_b"), ALU.add).then_inc(sem("h2_ready"), 1)
                yield
                dve.wait_ge(sem("scale_ready"), n)
                dve.wait_ge(sem("q2_ready"), n)
                for k in range(4, 8):
                    v.tensor_scalar(qt2[s][:, k * S:(k + 1) * S], p[:, k * S:(k + 1) * S], fs1[s][:, k:k + 1], fs1[s][:, XB + k:XB + k + 1],
                                    ALU.mult, ALU.add).then_inc(sem("q2t_dve"), 1)
                yield
                dve.wait_ge(sem("s2_ready"), n)
                sc = p[:, :].rearrange("p (a m) -> p a m", a=4)[:, :, 0:4 * C].rearrange("p a (h m) -> p a h m", h=4)
                link(v.tensor_reduce(neg_max[s][:, :].rearrange("p (a h) -> p a h", a=4), sc, AX.X, ALU.max, negate=True))
                split_max(link, s).then_inc(sem("m2_split"), 1)
                yield
                yield
                yield
                dve.wait_ge(sem("o2_ready"), n)
                o2 = p[:, :].rearrange("p (a m) -> p a m", a=4)[:, :, 0:4 * 65].rearrange("p a (h m) -> p a h m", h=4)
                link(v.reciprocal(rec[s][:, :].rearrange("p (a h) -> p a h", a=4), o2[:, :, :, XD]))
                for a in range(4):
                    r = v.tensor_tensor(heads(big[s][:, a * 256:(a + 1) * 256], 4), o2[:, a, :, 0:XD],
                                        rec[s][:, 4 * a:4 * a + 4].unsqueeze(2).broadcast_to([128, 4, XD]), ALU.mult)
                r.then_inc(sem("o2_normed"), 1)
                yield
                dve.wait_ge(sem("o2_turned"), n)
                v.tensor_copy(big[s][:, 1536:2048], p[:, BANK:2 * BANK]).then_inc(sem("o2t_dve"), 1)
                yield
                dve.wait_ge(sem("y2_ready"), n)
                link(v.tensor_tensor(zz[s][:, :], p[:, 2 * BANK:2 * BANK + D], xs[s][:, :], ALU.add))
                var(link, zz[s][:, :], s, "z2")
                norm(xs[s][:, :], zz[s][:, :], b, s, "z2").then_inc(sem("x2_ready"), 1)
                assert count[0] == LINKS["dve_first"], ("dve_first", count)
                yield

            def second(b, n, s):
                p = ps[s]
                link, count = link_on("dve_second", b)
                yield
                dve.wait_ge(sem("lg_ready"), n)
                link(v.tensor_scalar(lg[s][:, :], p[0:E, BANK:BANK + S], row("bg", E), None, ALU.add))
                v.tensor_reduce(esum[s][:, 0:1], lg[s][:, :], AX.X, ALU.max, negate=True).then_inc(sem("lg_max"), 1)
                dve.wait_ge(sem("lg_exp"), n)
                link(v.reciprocal(esum[s][:, 2:3], esum[s][:, 1:2]))
                link(v.tensor_scalar(prb[s][:, :], prb[s][:, :], esum[s][:, 2:3], None, ALU.mult), apart=True)
                for r in range(TOPK // 8):
                    src = prb[s] if r == 0 else left[s]
                    link(v.max(top8[s][:, :], src[:, :]), apart=True)
                    link(v.match_replace(left[s][:, :], top8[s][:, :], src[:, :], -1.0), apart=r < TOPK // 8 - 1)
                v.scalar_tensor_tensor(gate[s][:, :], left[s][:, :], 0.0, prb[s][:, :], ALU.is_lt, ALU.mult).then_inc(sem("gate_ready"), 1)
                yield
                dve.wait_ge(sem("gate_turned"), n)
                link(v.tensor_copy(gt[s][:, :], p[:, 2 * BANK:2 * BANK + E]))
                link(v.tensor_tensor(junk[s][:, 0:E], gt[s][:, :], row("b3"), ALU.mult))
                link(v.tensor_reduce(gb[s][:, :], junk[s][:, 0:E], AX.X, ALU.add))
                link(v.tensor_scalar(acc[s][:, 0:D], xs[s][:, :], gb[s][:, :], None, ALU.add))
                yield
                b8 = b * 8
                for e2 in range(STEPS):
                    if e2 >= 3:
                        dve.wait_ge(sem("e3_ready"), b8 + e2 - 2)
                        for e in (2 * e2 - 6, 2 * e2 - 5):
                            a = acc[s][:, (e % 2) * D:(e % 2 + 1) * D]
                            y = p[:, 2 * BANK + e % 2 * D:2 * BANK + (e % 2 + 1) * D]
                            if e == 1:
                                link(v.tensor_scalar(a, y, gt[s][:, e:e + 1], None, ALU.mult))
                            else:
                                link(v.scalar_tensor_tensor(a, y, gt[s][:, e:e + 1], a, ALU.mult, ALU.add))
                    yield
                link(v.tensor_tensor(zz[s][:, :], acc[s][:, 0:D], acc[s][:, D:2 * D], ALU.add))
                var(link, zz[s][:, :], s, "z3")
                link(norm(xs[s][:, :], zz[s][:, :], b, s, "z3"))
                square(xs[s], s, "r1")
                dve.wait_ge(ln_sem("r1", "rstd"), ln_count("r1", b))
                k = LNS["r1"]
                v.scalar_tensor_tensor(hs[s][:, :], xs[s][:, :], rstd[s][:, k:k + 1], row("rms1"), ALU.mult, ALU.mult).then_inc(sem("h4_ready"), 1)
                yield
                dve.wait_ge(sem("exp_r"), n)
                link(v.tensor_scalar(oo[s][:, :], oo[s][:, :], 1.0, None, ALU.add))
                link(v.reciprocal(oo[s][:, :], oo[s][:, :]))
                q4v = q4[s][:, :].rearrange("p (h a c) -> p h a c", h=H, a=4)
                k4v = k4[s][:, :].rearrange("p (h a c) -> p h a c", h=H, a=4)
                link(v.tensor_copy(q4v[:, :, 0::2, :], dups(heads(oo[s]))))
                v.tensor_tensor(q4v[:, :, 1::2, :], dups(heads(oo[s])), q4v[:, :, 0::2, :].bitcast(F), ALU.subtract).then_inc(sem("r4_split"), 1)
                yield
                dve.wait_ge(sem("k4_moved"), n)
                link(v.scalar_tensor_tensor(junk[s][:, :], junk[s][:, :], 0.5, junk[s][:, :], ALU.is_gt, ALU.mult))
                kk = heads(junk[s])
                big4 = big[s][:, 0:1024].rearrange("p (h i j) -> p h i j", h=H, i=HD)
                link(v.tensor_tensor(big4, kk.unsqueeze(2).broadcast_to([128, H, HD, HD]), kk.unsqueeze(3).broadcast_to([128, H, HD, HD]), ALU.is_gt))
                link(v.tensor_reduce(zz[s][:, :].rearrange("p (h c) -> p h c", h=H), big4, AX.X, ALU.add))
                link(v.scalar_tensor_tensor(junk[s][:, :], zz[s][:, :], 3.5, junk[s][:, :], ALU.is_lt, ALU.mult))
                link(v.tensor_copy(k4v[:, :, 0:2, :], dups(heads(junk[s]))))
                v.tensor_tensor(k4v[:, :, 2:4, :], dups(heads(junk[s])), k4v[:, :, 0:2, :].bitcast(F), ALU.subtract).then_inc(sem("k4_split"), 1)
                yield
                dve.wait_ge(sem("k4_turned"), n)
                v.tensor_copy(kt[s][:, :], p[:, 3 * BANK:4 * BANK]).then_inc(sem("k4t_ready"), 1)
                yield
                dve.wait_ge(sem("a4_ready"), n)
                v.tensor_tensor(prob[s][:, 2 * BANK:4 * BANK].rearrange("p (g q) -> p g q", q=S),
                                p[:, 2 * BANK:4 * BANK].rearrange("p (g q) -> p g q", q=S),
                                row("decay").unsqueeze(1).broadcast_to([128, 8, S]), ALU.mult).then_inc(sem("a4_dve"), 1)
                yield
                yield
                dve.wait_ge(sem("y4_mixed"), n)
                link(v.tensor_tensor(yy[s][:, :], p[:, BANK:BANK + D], xs[s][:, :], ALU.add))
                square(yy[s], s, "r2")
                dve.wait_ge(ln_sem("r2", "rstd"), ln_count("r2", b))
                k = LNS["r2"]
                v.scalar_tensor_tensor(hs[s][:, :], yy[s][:, :], rstd[s][:, k:k + 1], row("rms2"), ALU.mult, ALU.mult).then_inc(sem("h5_ready"), 1)
                yield
                yield
                dve.wait_ge(sem("one_plus_u"), n)
                hid, mid = big[s][:, 0:HID], big[s][:, HID:2 * HID]
                link(v.reciprocal(hid, hid))
                link(v.tensor_tensor(mid, p[:, 0:HID], hid, ALU.mult))
                v.tensor_tensor(mid, p[:, BANK:2 * BANK], mid, ALU.mult).then_inc(sem("mid_ready"), 1)
                yield
                dve.wait_ge(sem("down4_ready"), n)
                dve.wait_ge(sem("xx4"), n)
                link(v.tensor_tensor(zz[s][:, :], p[:, 2 * BANK:2 * BANK + D], xres[s][:, :], ALU.add))
                var(link, zz[s][:, :], s, "z4")
                norm(xs[s][:, :], zz[s][:, :], b, s, "z4").then_inc(sem("x4_ready"), 1)
                yield
                yield
                dve.wait_ge(sem("q5_ready"), n)
                link(v.tensor_tensor(oo[s][:, :], p[:, BANK:BANK + D], row("bq5"), ALU.add))
                q4v = q4[s][:, :].rearrange("p (h a c) -> p h a c", h=H, a=4)
                link(v.tensor_copy(q4v[:, :, 0::2, :], dups(heads(oo[s]))))
                v.tensor_tensor(q4v[:, :, 1::2, :], dups(heads(oo[s])), q4v[:, :, 0::2, :].bitcast(F), ALU.subtract).then_inc(sem("q5_split"), 1)
                yield
                yield
                dve.wait_ge(sem("s5_ready"), n)
                sc = p[:, :].rearrange("p (a m) -> p a m", a=4)[:, :, 0:4 * CE].rearrange("p a (h m) -> p a h m", h=4)[:, :, :, 0:C]
                link(v.tensor_reduce(neg_max[s][:, :].rearrange("p (a h) -> p a h", a=4), sc, AX.X, ALU.max, negate=True))
                split_max(link, s).then_inc(sem("m5_split"), 1)
                yield
                yield
                yield
                dve.wait_ge(sem("o5_ready"), n)
                o = heads(p[:, 0:H * 9])
                link(v.tensor_copy(den[s][:, :], o[:, :, HD]))
                weighted(link, o, s, HD, "o5_normed")
                yield
                yield
                dve.wait_ge(sem("y5_ready"), n)
                dve.wait_ge(sem("xbias5"), n)
                link(v.tensor_tensor(zz[s][:, :], p[:, BANK:BANK + D], xbias[s][:, :], ALU.add))
                var(link, zz[s][:, :], s, "z5")
                norm(xs[s][:, :], zz[s][:, :], b, s, "z5").then_inc(sem("x5_ready"), 1)
                yield
                yield
                dve.wait_ge(sem("y6_ready"), n)
                if type(b) is int and b == B - 1:
                    dve.wait_ge(sem("stored"), 16 * (B - 2))
                link(v.tensor_tensor(zz[s][:, :], p[:, BANK:BANK + D], xs[s][:, :], ALU.add))
                var(link, zz[s][:, :], s, "z6")
                yield
                norm(res[s][:, :], zz[s][:, :], b, s, "z6").then_inc(sem("out_ready"), 1)
                assert count[0] == LINKS["dve_second"], ("dve_second", count)
                yield

            def square(t, s, name):
                k = LNS[name]
                v.tensor_tensor_reduce(out=junk[s][:, :], in0=t[:, :], in1=t[:, :], scale=1.0, scalar=0.0, op0=ALU.mult, op1=ALU.add,
                                       accum_out=mv[s][:, 2 * k + 1:2 * k + 2]).then_inc(ln_sem(name, "var"), 1)

            dve.wait_ge(sem("whole_loaded"), 16)
            ternary()
            whole_run(dve, first, second)

        @block.tensor
        def _(pe):
            mm = pe.matmul

            def mm3(out_, left, right, start=True, stop=True, **kw):
                mm(out_, left[0], right[0], start=start, stop=False, **kw)
                mm(out_, left[0], right[1], start=False, stop=False, **kw)
                return mm(out_, left[1], right[0], start=False, stop=stop, **kw)

            def turn(out_, src, rows=128):
                return pe.transpose(out_.bitcast(R), src, ident_r[0:rows, 0:rows])

            def turn_pair(p, src):
                turn(p[:, 0:D], src[:, 0:D])
                return turn(p[:, D:2 * D], src[:, D:2 * D])

            def pair(t):
                return t[:, 0:D], t[:, D:2 * D]

            def wpair(name, a=0, b=None):
                return split_w(name, 0, a, b), split_w(name, 1, a, b)

            def turn_heads(p, src, rows=128):
                for g in range(G4):
                    r = turn(p[:, g * rows:(g + 1) * rows], src[:, g * 128:(g + 1) * 128], rows)
                return r

            def ready(name, n):
                pe.wait_ge(sem(name), n)

            ready("ident_ready", 2)
            ready("ones_set", 1)
            ready("t_abs", 1)
            mm(ps[1][:, 0:1], ones[:, :], t_abs[:, :], start=True, stop=True).then_inc(sem("t_sum"), 1)
            ready("w_split", len(CHUNKS))
            ready("tern_ready", 1)
            ready("whole_loaded", 16)

            def first(b, n, s):
                p = ps[s]
                pe.wait_ge(rows_sem("x1", "split"), rows_count("x1", b))
                turn_pair(p, xp[s]).then_inc(rows_sem("x1", "turned"), 1)
                yield
                pe.wait_ge(rows_sem("x1", "back"), rows_count("x1", b))
                mm3(p[:, BANK:BANK + 3 * D], pair(xt[s]), wpair("qkv1")).then_inc(sem("qkv1_ready"), 1)
                yield
                ready("qk1_split", n)
                turn_heads(p[:, 2 * BANK:3 * BANK], q4[s]).then_inc(sem("q1_turned"), 1)
                turn_heads(p[:, 3 * BANK:4 * BANK], k4[s]).then_inc(sem("k1_turned"), 1)
                yield
                ready("cn_split", n)
                ready("c_used", n)
                for k in range(4):
                    r = turn(p[:, k * CE:(k + 1) * CE], cp[s][:, k * D:(k + 1) * D], CE)
                r.then_inc(sem("c_turned"), 1)
                yield
                ready("q1t_ready", n)
                ready("k1t_ready", n)
                ready("ct_ready", n)
                for g in range(G4):
                    for j in range(4):
                        at = slice(32 * j, 32 * j + 32)
                        r = mm(p[:, j * BANK + g * S:j * BANK + (g + 1) * S], kt[s][at, g * S:(g + 1) * S], qt[s][at, g * S:(g + 1) * S], start=True, stop=True)
                r.then_inc(sem("a1_ready"), 1)
                yield
                ready("p1_act", n)
                ready("p1_dve", n)
                for h in range(H):
                    j, g = h % 4, h // 4
                    r = mm(p[:, h * 9:(h + 1) * 9], prob[s][:, (j * 4 + g) * S:(j * 4 + g + 1) * S], v9[s][:, h * 9:(h + 1) * 9], start=True, stop=True)
                r.then_inc(sem("o1_ready"), 1)
                cpair = lambda k: (ct[s][:, 2 * k * CE:(2 * k + 1) * CE], ct[s][:, (2 * k + 1) * CE:(2 * k + 2) * CE])
                mm3(p[0:CE, BANK:BANK + 2 * D], cpair(1), wpair("kv5")).then_inc(sem("kv5_ready"), 1)
                for k in range(XB):
                    at = (2 + k // 4) * BANK + (k % 4) * CE
                    r = mm3(p[:, at:at + CE], wpair("k2", k * 128, (k + 1) * 128), cpair(0))
                r.then_inc(sem("k2_ready"), 1)
                yield
                ready("o1_normed", n)
                pe.transpose(p[:, 0:D], oo[s][:, :], row("ident")).then_inc(sem("o1_turned"), 1)
                ready("k2t_ready", n)
                for k in range(2):
                    r = mm3(p[0:CE, (2 + k) * BANK:(3 + k) * BANK], cpair(0), wpair("v2", k * BANK, (k + 1) * BANK))
                r.then_inc(sem("v2_ready"), 1)
                yield
                ready("o1t_ready", n)
                mm(p[:, 0:D], ot[s][:, :], whole_w("out1"), start=True, stop=True).then_inc(sem("y1_ready"), 1)
                ready("v5_ready", n)
                ready("k5_split", n)
                turn_heads(p[:, BANK:2 * BANK], k45[s], CE).then_inc(sem("k5_turned"), 1)
                yield
                pe.wait_ge(rows_sem("h2", "split"), rows_count("h2", b))
                turn_pair(p, xp[s]).then_inc(rows_sem("h2", "turned"), 1)
                yield
                pe.wait_ge(rows_sem("h2", "back"), rows_count("h2", b))
                ready("k5t_ready", n)
                for k in range(XB):
                    r = mm3(p[:, k * S:(k + 1) * S], wpair("q2", k * 128, (k + 1) * 128), pair(xt[s]))
                r.then_inc(sem("q2_ready"), 1)
                yield
                ready("q2t_act", n * 4)
                ready("q2t_dve", n * 4)
                ready("v2_act", n)
                ready("v2_dve", n)
                for k in range(XB):
                    for par in range(2):
                        at = slice(64 * par, 64 * par + 64)
                        c0 = (k // 4 * 2 + par) * BANK + (k % 4) * C
                        r = mm(p[:, c0:c0 + C], qt2[s][at, k * S:(k + 1) * S], kt2[s][at, k * CE:k * CE + C], start=True, stop=True)
                r.then_inc(sem("s2_ready"), 1)
                yield
                ready("m2_split", n)
                turn(p[:, 0:S], nm[s][:, :]).then_inc(sem("m2_turned"), 1)
                yield
                ready("m2t_ready", n)
                for hf in range(2):
                    for k in range(4 * hf, 4 * hf + 4):
                        for par in range(2):
                            at = slice(64 * par, 64 * par + 64)
                            c0 = (hf * 2 + par) * BANK + (k % 4) * S
                            mm(p[0:C, c0:c0 + S], kt2[s][at, k * CE:k * CE + C], qt2[s][at, k * S:(k + 1) * S], start=(k % 4 == 0), stop=False, skip_group_check=True)
                    for k in range(4 * hf, 4 * hf + 4):
                        for par in range(2):
                            i = (hf * 2 + par) * 4 + k % 4
                            c0 = (hf * 2 + par) * BANK + (k % 4) * S
                            at = slice(i // 4 * 32, i // 4 * 32 + 32)
                            r = mm(p[0:C, c0:c0 + S], pick_r[at, i * CE:i * CE + C], nmt[s][at, :], start=False, stop=(k % 4 == 3), skip_group_check=True)
                    r.then_inc(sem("s2_first" if hf == 0 else "s2_last"), 1)
                yield
                ready("p2_first", n)
                ready("p2_last", n)
                for i in range(XH):
                    par, k = i // 4 % 2, i // 8 * 4 + i % 4
                    c0 = i * S
                    o0 = (i // 4) * BANK + (i % 4) * 65
                    r = mm(p[:, o0:o0 + 65], prob[s][0:C, c0:c0 + S], v65[s][0:C, (2 * k + par) * 65:(2 * k + par + 1) * 65], start=True, stop=True)
                r.then_inc(sem("o2_ready"), 1)
                yield
                ready("o2_normed", n)
                for k in range(XB):
                    r = pe.transpose(p[:, k * S:(k + 1) * S], big[s][:, k * 128:(k + 1) * 128], row("ident"))
                r.then_inc(sem("o2_turned"), 1)
                yield
                ready("o2t_act", n)
                ready("o2t_dve", n)
                for k in range(XB):
                    r = mm(p[:, 2 * BANK:2 * BANK + D], big[s][:, 1024 + k * S:1024 + (k + 1) * S], whole_w("out2", k * D, (k + 1) * D), start=(k == 0), stop=(k == XB - 1))
                r.then_inc(sem("y2_ready"), 1)
                yield

            def second(b, n, s):
                p = ps[s]
                pe.wait_ge(rows_sem("x3", "split"), rows_count("x3", b))
                turn_pair(p, xp[s]).then_inc(rows_sem("x3", "turned"), 1)
                yield
                pe.wait_ge(rows_sem("x3", "back"), rows_count("x3", b))
                mm3(p[:, BANK:BANK + S], wpair("gate"), pair(xt[s])).then_inc(sem("lg_ready"), 1)
                yield
                yield
                b8 = b * 8
                for e2 in range(STEPS):
                    if e2 < 8:
                        for e in (2 * e2, 2 * e2 + 1):
                            c0 = e2 % 2 * 3 * BANK + e % 2 * S
                            r = mm3(p[:, c0:c0 + S], wpair("exp1", e * D, (e + 1) * D), pair(xt[s]))
                        r.then_inc(sem("e1_ready"), 1)
                    if e2 == 2:
                        wait_apart(pe, sem("gate_ready"), n)
                        pe.transpose(p[:, 2 * BANK:2 * BANK + E], gate[s][:, :], row("ident", E)[:, 0:E]).then_inc(sem("gate_turned"), 1)
                    if e2 >= 3:
                        ready("e2_relu", b8 + e2 - 2)
                        pe.wait_ge(sem("dve_second"), b * LINKS["dve_second"] + GATE_LINKS + (0 if e2 == 3 else E3_LINKS - GATE_LINKS + 2 * (e2 - 3)))
                        for e in (2 * e2 - 6, 2 * e2 - 5):
                            r = mm(p[:, 2 * BANK + e % 2 * D:2 * BANK + (e % 2 + 1) * D], big[s][:, e * S:(e + 1) * S], whole_w("exp3", e * D, (e + 1) * D), start=True, stop=True)
                        r.then_inc(sem("e3_ready"), 1)
                    if 1 <= e2 < 9:
                        if e2 == 1:
                            ready("lg_max", n)
                        else:
                            ready("e2_relu", b8 + e2 - 1)
                        ready("e1_relu", b8 + e2)
                        for e in (2 * e2 - 2, 2 * e2 - 1):
                            r = mm(p[:, BANK + e % 2 * S:BANK + (e % 2 + 1) * S], whole_w("exp2", e * D, (e + 1) * D), prob[s][:, e * S:(e + 1) * S], start=True, stop=True)
                        r.then_inc(sem("e2_ready"), 1)
                    yield
                pe.wait_ge(rows_sem("h4", "split"), rows_count("h4", b))
                turn_pair(p, xp[s]).then_inc(rows_sem("h4", "turned"), 1)
                yield
                pe.wait_ge(rows_sem("h4", "back"), rows_count("h4", b))
                mm3(p[:, BANK:BANK + 3 * D], pair(xt[s]), wpair("rkv4")).then_inc(sem("rkv4_ready"), 1)
                yield
                ready("r4_split", n)
                turn_heads(p[:, 2 * BANK:3 * BANK], q4[s]).then_inc(sem("r4_turned"), 1)
                yield
                ready("k4_split", n)
                turn_heads(p[:, 3 * BANK:4 * BANK], k4[s]).then_inc(sem("k4_turned"), 1)
                yield
                ready("r4t_ready", n)
                ready("k4t_ready", n)
                ready("v4_ready", n)
                for g in range(G4):
                    for j in range(4):
                        at = slice(32 * j, 32 * j + 32)
                        r = mm(p[:, j * BANK + g * S:j * BANK + (g + 1) * S], kt[s][at, g * S:(g + 1) * S], qt[s][at, g * S:(g + 1) * S], start=True, stop=True)
                r.then_inc(sem("a4_ready"), 1)
                yield
                ready("a4_decayed", n)
                ready("a4_dve", n)
                for h in range(H):
                    j, g = h % 4, h // 4
                    r = mm(p[:, h * HD:(h + 1) * HD], prob[s][:, (j * 4 + g) * S:(j * 4 + g + 1) * S], v9[s][:, h * 9:h * 9 + HD], start=True, stop=True)
                r.then_inc(sem("y4_ready"), 1)
                yield
                ready("y4_moved", n)
                pe.transpose(p[:, 0:D], oo[s][:, :], row("ident")).then_inc(sem("y4_turned"), 1)
                ready("y4t_ready", n)
                mm(p[:, BANK:BANK + D], ot[s][:, :], whole_w("out4"), start=True, stop=True).then_inc(sem("y4_mixed"), 1)
                yield
                pe.wait_ge(rows_sem("h5", "split"), rows_count("h5", b))
                turn_pair(p, xp[s]).then_inc(rows_sem("h5", "turned"), 1)
                yield
                pe.wait_ge(rows_sem("h5", "back"), rows_count("h5", b))
                for k in range(8):
                    c0 = k * 128
                    r = mm3(p[:, c0:c0 + S], wpair("up4", c0, c0 + 128), pair(xt[s]))
                    if k == 7:
                        r.then_inc(sem("up4_ready"), 1)
                yield
                ready("mid_ready", n)
                for k in range(4):
                    r = mm(p[:, 2 * BANK:2 * BANK + D], big[s][:, HID + k * S:HID + (k + 1) * S], whole_w("down4", k * D, (k + 1) * D), start=(k == 0), stop=(k == 3))
                r.then_inc(sem("down4_ready"), 1)
                yield
                pe.wait_ge(rows_sem("x5", "split"), rows_count("x5", b))
                turn_pair(p, xp[s]).then_inc(rows_sem("x5", "turned"), 1)
                yield
                pe.wait_ge(rows_sem("x5", "back"), rows_count("x5", b))
                mm3(p[:, BANK:BANK + D], pair(xt[s]), wpair("q5")).then_inc(sem("q5_ready"), 1)
                yield
                ready("q5_split", n)
                turn_heads(p[:, 2 * BANK:3 * BANK], q4[s]).then_inc(sem("q5_turned"), 1)
                yield
                ready("q5t_ready", n)
                for g in range(G4):
                    for j in range(4):
                        at = slice(32 * j, 32 * j + 32)
                        r = mm(p[:, j * BANK + g * CE:j * BANK + (g + 1) * CE], qt[s][at, g * S:(g + 1) * S], kt5[s][at, g * CE:(g + 1) * CE], start=True, stop=True)
                r.then_inc(sem("s5_ready"), 1)
                yield
                ready("m5_split", n)
                turn(p[:, 0:S], nm[s][:, :]).then_inc(sem("m5_turned"), 1)
                yield
                ready("m5t_ready", n)
                for g in range(G4):
                    for j in range(4):
                        at = slice(32 * j, 32 * j + 32)
                        mm(p[0:C, j * BANK + g * S:j * BANK + (g + 1) * S], kt5[s][at, g * CE:g * CE + C], qt[s][at, g * S:(g + 1) * S], start=(g == 0), stop=False, skip_group_check=True)
                for g in range(G4):
                    for j in range(4):
                        at = slice(32 * j, 32 * j + 32)
                        i = j * 4 + g
                        r = mm(p[0:C, j * BANK + g * S:j * BANK + (g + 1) * S], pick_r[at, i * CE:i * CE + C], nmt[s][at, :], start=False, stop=(g == 3), skip_group_check=True)
                r.then_inc(sem("s5t_ready"), 1)
                yield
                ready("p5_ready", n * 2)
                for h in range(H):
                    j, g = h % 4, h // 4
                    r = mm(p[:, h * 9:(h + 1) * 9], prob[s][0:C, (j * 4 + g) * S:(j * 4 + g + 1) * S], v95[s][0:C, h * 9:(h + 1) * 9], start=True, stop=True)
                r.then_inc(sem("o5_ready"), 1)
                yield
                ready("o5_normed", n)
                pe.transpose(p[:, 0:D], oo[s][:, :], row("ident")).then_inc(sem("o5_turned"), 1)
                yield
                ready("o5t_ready", n)
                mm(p[:, BANK:BANK + D], ot[s][:, :], whole_w("out5"), start=True, stop=True).then_inc(sem("y5_ready"), 1)
                yield
                ready("x5_ready", n)
                pe.transpose(p[:, 0:D], xs[s][:, :], row("ident")).then_inc(sem("x6_turned"), 1)
                yield
                ready("x6t_ready", n)
                mm(p[:, BANK:BANK + D], ot[s][:, :], whole_w("tern6"), start=True, stop=True).then_inc(sem("y6_ready"), 1)
                yield
                yield

            whole_run(pe, first, second)


GATE_LINKS, E3_LINKS = 12, 15


def kernel(**inputs):
    import concourse.bacc as bacc
    from concourse.bass_utils import run_bass_kernel_spmd

    a = {k: np.asarray(v) for k, v in inputs.items()}
    f = np.float32

    def heads_apart(w, parts):
        return w.reshape(D, H, parts, HD).transpose(0, 2, 1, 3).reshape(D, parts * D)

    kv = a["L0_xattn_Wkv"]
    experts = lambda w: w.transpose(1, 0, 2).reshape(D, E * D)
    out2 = a["L0_xattn_Wout"].reshape(2, 4, 2, XD, D).transpose(0, 2, 1, 3, 4).reshape(XB, 128, D).transpose(1, 0, 2).reshape(128, XB * D)
    split = dict(
        qkv1=heads_apart(a["L0_attn_w_qkv"], 3), k2=kv[:, :XH * XD], v2=kv[:, XH * XD:],
        kv5=np.concatenate([a["L1_xattn_wk_w"].T, a["L1_xattn_wv_w"].T], 1), q2=a["L0_xattn_Wq"],
        gate=np.concatenate([a["L0_ffn_Wg"], np.zeros((D, 128 - E), f)], 1), exp1=experts(a["L0_ffn_w1"]),
        rkv4=np.concatenate([a["L1_attn_Wr"], a["L1_attn_Wk"], a["L1_attn_Wv"]], 1),
        up4=np.concatenate([a["L1_attn_w1"], a["L1_attn_w2"]], 1), q5=a["L1_xattn_wq_w"].T)
    whole = dict(
        out1=a["L0_attn_w_out"], out2=out2, exp2=experts(a["L0_ffn_w2"]), exp3=experts(a["L0_ffn_w3"]), out4=a["L1_attn_Wo"],
        down4=a["L1_attn_w3"].reshape(4, 128, D).transpose(1, 0, 2).reshape(128, HID), out5=a["L1_xattn_dense_w"].T,
        tern6=a["L1_ffn_weight"].T)
    t = np.arange(S)
    lag = t[None, :] - t[:, None]
    decay = np.where(lag >= 0, DECAY ** np.maximum(lag, 0).astype(np.float64), 0.0).astype(f)
    pick = np.zeros((4, 2, XH, XH, CE), f)
    for i in range(XH):
        pick[:, :, i, i] = 1.0
    rows = lambda v: np.broadcast_to(v.reshape(1, -1), (128, v.size))
    const = dict(
        ident=np.eye(128, dtype=f), decay=decay, b_out=rows(a["L0_attn_b_out"]), gamma=rows(a["L0_attn_gamma"]),
        beta=rows(a["L0_attn_beta"]), ln1_w=rows(a["L0_xattn_ln1_w"]), ln1_b=rows(a["L0_xattn_ln1_b"]), ln2_w=rows(a["L0_xattn_ln2_w"]),
        ln2_b=rows(a["L0_xattn_ln2_b"]), rms1=rows(a["L1_attn_norm1_w"]), rms2=rows(a["L1_attn_norm2_w"]), bk5=rows(a["L1_xattn_wk_b"]),
        bv5=rows(a["L1_xattn_wv_b"]), bq5=rows(a["L1_xattn_wq_b"]), bd5=rows(a["L1_xattn_dense_b"]), b1=rows(a["L0_ffn_b1"]),
        b2=rows(a["L0_ffn_b2"]), b3=rows(a["L0_ffn_b3"]),
        bg=np.concatenate([a["L0_ffn_bg"].reshape(E, 1), np.zeros((128 - E, 1), f)], 0))
    fs = a["fside_Bx16_0"].reshape(B, XB, 2)
    fs = np.repeat(fs.transpose(0, 2, 1), XD, axis=1)
    arrays = {
        "x": a["x"], "ctx": a["ctx_1024"], "fside": fs,
        "w_split": np.concatenate([split[n] for n, _ in SPLIT], 1),
        "w_whole": np.concatenate([whole[n] for n, _ in WHOLE], 1),
        "const": np.concatenate([const[n] for n, _ in CONST], 1), "picker": pick.reshape(128, XH * CE),
    }
    arrays = {k: np.ascontiguousarray(v) for k, v in arrays.items()}
    nc = bacc.Bacc("TRN2", target_bir_lowering=False, num_devices=1)
    args = [nc.dram_tensor(k, v.shape, mybir.dt.float32, kind="ExternalInput").ap() for k, v in arrays.items()]
    out = nc.dram_tensor("decoded", (B, S, D), mybir.dt.float32, kind="ExternalOutput").ap()
    decoder(nc, *args, out)
    r = run_bass_kernel_spmd(nc, [arrays], core_ids=[0])
    return r.results[0]["decoded"]
```

```python
from contextlib import ExitStack

import numpy as np

import concourse.bass as bass
from concourse import mybir

B, S, D = 16, 128, 128
C, CE = 77, 78
H, HD = 16, 8
XH, XD = 16, 64
XB = XH * XD // 128
E, TOPK = 16, 32
HID = 512
G4 = H // 4
DECAY = 0.9
LN_EPS, KERN_EPS = 1e-5, 1e-6
BANK = 512
SLOTS = 4

WEIGHTS = [("qkv1", 3 * D), ("k2", XH * XD), ("v2", XH * XD), ("kv5", 2 * D), ("out1", D), ("q2", XH * XD),
           ("out2", XB * D), ("gate", E), ("exp1", E * D), ("exp2", E * D), ("exp3", E * D), ("rkv4", 3 * D),
           ("out4", G4 * D), ("up4", 2 * HID), ("down4", HID), ("q5", D), ("out5", D), ("tern6", D)]
CONST = [("ident", 128), ("decay", 128), ("pick", XH), ("b_out", D), ("gamma", D), ("beta", D),
         ("ln1_w", D), ("ln1_b", D), ("ln2_w", D), ("ln2_b", D), ("rms1", D), ("rms2", D), ("bk5", D),
         ("bv5", D), ("bq5", D), ("bd5", D), ("b1", E), ("b2", E), ("b3", E), ("bg", 1)]
PIECES = ["qkv1", "out1", "out2", "exp1", "exp3", "tern6"]


def offsets(parts):
    at, out = 0, {}
    for name, n in parts:
        out[name] = (at, at + n)
        at += n
    return out, at


WEIGHT_AT, WEIGHT_COLS = offsets(WEIGHTS)
CONST_AT, CONST_COLS = offsets(CONST)

ORDERS = {
    "pool": "033330220330103",
    "act": "22013202310232033213230211203302200332133",
    "dve": "223003122013202321023230333300221222201201202333101303",
    "pe": "22210203321103303313212023302332231323130010203002321302032020120103133333321133",
}
LINKS = {"dve": [15, 6, 24, 13], "pool": [5, 1, 2, 4]}


def decoder(nc, rows_in, weights, const, out):
    F, R = mybir.dt.float32, mybir.dt.float32r
    ALU, ACT, AX = mybir.AluOpType, mybir.ActivationFunctionType, mybir.AxisListType
    held = ExitStack()
    with held:
        def sb(name, cols, dt=F, rows=128):
            return held.enter_context(nc.sbuf_tensor(name, [rows, cols], dt))

        def slots(name, cols, dt=F, rows=128):
            return [sb(f"{name}{s}", cols, dt, rows) for s in range(SLOTS)]

        sems = {}

        def sem(name):
            if name not in sems:
                sems[name] = held.enter_context(nc.semaphore(name))
            return sems[name]

        wts = sb("wts", WEIGHT_COLS)
        cst = sb("cst", CONST_COLS)
        ident_r, pick_r = sb("ident_r", 128, R), sb("pick_r", XH, R)
        half_exp = sb("half_exp", 1)
        t_abs, t_scale, t_half, t_neg = sb("t_abs", 1), sb("t_scale", 1), sb("t_half", 1), sb("t_neg", 1)

        inputs = slots("inputs", 2 * D + XB)
        xin, cin, fs = [t[:, 0:D] for t in inputs], [t[0:C, D:2 * D] for t in inputs], [t[:, 2 * D:2 * D + XB] for t in inputs]
        fs1 = slots("fs1", 2 * XB)
        xs = slots("xs", D)
        xbias, xres = slots("xbias", D), slots("xres", D)
        yy, zz = slots("yy", D), slots("zz", D)
        res = slots("res", D)
        xt = slots("xt", D)
        oo = slots("oo", D)
        junk = slots("junk", D)
        ct = slots("ct", 2 * C)
        q4, k4 = slots("q4", 4 * D, R), slots("k4", 4 * D, R)
        qt, kt = slots("qt", 4 * D, R), q4
        kt5 = slots("kt5", 4 * CE, R)
        v9, v95 = slots("v9", (H - 1) * 9 + 32), slots("v95", (H - 1) * 9 + 32, rows=C)
        v65 = slots("v65", XH * 65, rows=C)
        kt2 = slots("kt2", XB * C)
        prob = slots("prob", H * S)
        big = slots("big", XH * XD)
        sums = [t[:, 0:4 * D] for t in big]
        qt2 = big
        den, rec, neg_max = slots("den", H), slots("rec", H), slots("neg_max", H)
        nm, nmt = slots("nm", 128, R), slots("nmt", S, R)
        stats, mv, veps, rstd = slots("stats", 6), slots("mv", 2 * 11), slots("veps", 1), slots("rstd", 11)
        gb, esum, top8, gt = slots("gb", 1), slots("esum", 3, rows=E), slots("top8", 8, rows=E), slots("gt", E)
        ps = [held.enter_context(nc.psum_tensor(f"ps{s}", [128, 2 * BANK], F)) for s in range(SLOTS)]

        LN = [["ctx", "y1", "z1", "q2"], ["z2"], ["z3", "r1"], ["r2", "z4", "z5", "z6"]]
        LN_AT = {n: i for i, n in enumerate(n for part in LN for n in part)}

        def ln_sem(name, what):
            return sem(f"{what}{[name in part for part in LN].index(True)}")

        def ln_count(name, b):
            order = next(part for part in LN if name in part)
            return b * len(order) + order.index(name) + 1

        def loads(b, s):
            return b * (16 // SLOTS) + 16 - s * (16 // SLOTS)

        def weight(name, a=0, b=None):
            at = WEIGHT_AT[name]
            return wts[:, at[0] + a:at[0] + b if b else at[1]]

        def row(name, rows=128):
            at = CONST_AT[name]
            return cst[0:rows, at[0]:at[1]]

        def heads(t, n=H, rows=128):
            return t[0:rows, :].rearrange("p (h c) -> p h c", h=n)

        def by_nine(t, rows=128):
            return t[0:rows, 0:H * 9].rearrange("p (h c) -> p h c", h=H)[:, :, 0:HD]

        def parts(t, rows=128):
            return t[0:rows, :].rearrange("p (h a c) -> p h a c", h=H, a=4)

        def wait_apart(eng, semaphore, value):
            if type(value) is not int:
                value = eng.to_reg(value)
                eng.wait_ge(sem("const_loaded"), 16)
            eng.wait_ge(semaphore, value)

        block = held.enter_context(nc.Block())

        def linker(eng, who, q, b):
            count, total = [0], LINKS[who][q]
            base = b * total if type(b) is int else eng.snap(b * total)

            def link(ins, apart=False):
                count[0] += 1
                ins.then_inc(sem(f"{who}_link{q}"), 1)
                if apart:
                    wait_apart(eng, sem(f"{who}_link{q}"), base + count[0])
                else:
                    eng.wait_ge(sem(f"{who}_link{q}"), base + count[0])

            def finish():
                assert count[0] == total, (who, q, count[0])
            return link, finish

        def step(who, quarters, batches):
            running = {q: quarters[q](*batches[q]) for q in batches}
            for q in map(int, ORDERS[who]):
                if q in running:
                    next(running[q])
            for q, rest in running.items():
                assert next(rest, None) is None, ("a phase is left over", who, q)

        def whole_run(eng, who, quarters, before_last_quarters=None):
            def static(t):
                return {q: (t - q, t - q + 1, (t - q) % SLOTS) for q in range(4) if 0 <= t - q < B}
            for t in range(3):
                step(who, quarters, static(t))
            if before_last_quarters:
                before_last_quarters()
            with eng.Fori(0, (B - 4) // SLOTS) as i:
                first = eng.snap(i * SLOTS)
                nth = [first] + [eng.snap(first + k) for k in range(1, 8)]
                for u in range(SLOTS):
                    step(who, quarters, {q: (nth[3 + u - q], nth[4 + u - q], (3 + u - q) % SLOTS) for q in range(4)})
            for t in range(B - 1, B + 3):
                step(who, quarters, static(t))

        @block.sync
        def _(sp):
            def load(b, s):
                sp.dma_start(inputs[s][:, :], rows_in[bass.ds(b, 1), :, :].rearrange("b p n -> (b p) n")).then_inc(sem(f"x_loaded{s}"), 16)

            def store(b, s):
                sp.dma_start(out[bass.ds(b, 1), :, :].rearrange("b p n -> (b p) n"), res[s][:, :]).then_inc(sem("stored"), 16)

            load(0, 0)
            sp.dma_start(cst[:, :], const).then_inc(sem("const_loaded"), 16)
            at = 0
            for k, name in enumerate(PIECES):
                end = WEIGHT_AT[name][1]
                sp.dma_start(wts[:, at:end], weights[:, at:end]).then_inc(sem(f"w_loaded{k}"), 16)
                at = end
                if k < SLOTS - 1:
                    load(k + 1, k + 1)
            for t in range(3):
                sp.wait_ge(sem("x_used"), t + 1)
                sp.wait_ge(sem("f_used"), t + 1)
                sp.wait_ge(sem("c_turned"), t + 1)
                load(t + SLOTS, t)
            with sp.Fori(0, B // SLOTS - 2) as i:
                first = sp.snap(i * SLOTS)
                nth = [first] + [sp.snap(first + k) for k in range(1, 11)]
                stored = [sp.snap(first * 16 + 16 * (u + 1)) for u in range(SLOTS)]
                for u in range(SLOTS):
                    wait_apart(sp, sem("out_ready"), nth[u + 1])
                    store(nth[u], u)
                    wait_apart(sp, sem("stored"), stored[u])
                    sp.wait_ge(sem("x_used"), nth[u + 4])
                    sp.wait_ge(sem("f_used"), nth[u + 4])
                    wait_apart(sp, sem("c_turned"), nth[u + 4])
                    load(nth[u + 7], (u + 3) % SLOTS)
            for b in range(B - 2 * SLOTS, B):
                sp.wait_ge(sem("out_ready"), b + 1)
                store(b, b % SLOTS)
                sp.wait_ge(sem("stored"), 16 * (b + 1))
                if b + 7 < B:
                    sp.wait_ge(sem("x_used"), b + 4)
                    sp.wait_ge(sem("f_used"), b + 4)
                    sp.wait_ge(sem("c_turned"), b + 4)
                    load(b + 7, (b + 3) % SLOTS)

        @block.gpsimd
        def _(pool):
            pool.memset(half_exp[:, :], -0.5)
            for s in range(SLOTS):
                pool.memset(v9[s][:, :], 1.0)
                pool.memset(v95[s][:, :], 1.0)
                r = pool.memset(v65[s][:, :], 1.0)
            r.then_inc(sem("ones_set"), 1)
            pool.wait_ge(sem("ones_set"), 1)
            pool.wait_ge(sem("const_loaded"), 16)

            def inv_sqrt(link, b, s, name, scale=1.0, rows=128):
                k = LN_AT[name]
                wait_apart(pool, ln_sem(name, "var"), ln_count(name, b))
                link(pool.tensor_scalar(veps[s][0:rows, :], mv[s][0:rows, 2 * k + 1:2 * k + 2], scale, LN_EPS, ALU.mult, ALU.add), apart=True)
                pool.tensor_tensor(out=rstd[s][0:rows, k:k + 1], in0=veps[s][0:rows, :], in1=half_exp[0:rows, :], op=ALU.pow).then_inc(ln_sem(name, "rstd"), 1)

            def q0(b, n, s):
                link, finish = linker(pool, "pool", 0, b)
                pool.wait_ge(sem(f"x_loaded{s}"), loads(b, s))
                pool.tensor_tensor(out=xbias[s][:, :], in0=xin[s][:, :], in1=row("b_out"), op=ALU.add)
                pool.tensor_tensor(out=xres[s][:, :], in0=xin[s][:, :], in1=row("beta"), op=ALU.add).then_inc(sem("x_used"), 1)
                inv_sqrt(link, b, s, "ctx", rows=C)
                pool.tensor_copy(fs1[s][:, XB:2 * XB], fs[s][:, :])
                pool.tensor_scalar(fs1[s][:, 0:XB], fs[s][:, :], 1.0, None, ALU.add).then_inc(sem("f_used"), 1)
                yield
                wait_apart(pool, sem("kb_ready"), n)
                kv = heads(zz[s], rows=C).unsqueeze(2).broadcast_to([C, H, 2, HD])
                k5 = parts(k4[s], C)
                link(pool.tensor_copy(k5[:, :, 0:2, :], kv))
                pool.tensor_tensor(out=k5[:, :, 2:4, :], in0=kv, in1=k5[:, :, 0:2, :].bitcast(F), op=ALU.subtract).then_inc(sem("k5_split"), 1)
                yield
                inv_sqrt(link, b, s, "y1")
                yield
                inv_sqrt(link, b, s, "z1")
                yield
                inv_sqrt(link, b, s, "q2")
                yield
                finish()

            def q1(b, n, s):
                link, finish = linker(pool, "pool", 1, b)
                inv_sqrt(link, b, s, "z2")
                yield
                finish()

            def q2(b, n, s):
                link, finish = linker(pool, "pool", 2, b)
                inv_sqrt(link, b, s, "z3")
                yield
                inv_sqrt(link, b, s, "r1", 1.0 / D)
                yield
                finish()

            def q3(b, n, s):
                link, finish = linker(pool, "pool", 3, b)
                for half in range(2):
                    pool.wait_ge(sem("a4_moved"), b * 2 + half + 1)
                    p4 = prob[s][:, 2 * half * BANK:(2 * half + 1) * BANK].rearrange("p (g q) -> p g q", q=S)
                    pool.tensor_tensor(out=p4, in0=p4, in1=row("decay").unsqueeze(1).broadcast_to([128, G4, S]), op=ALU.mult).then_inc(sem("a4_decayed"), 1)
                    yield
                inv_sqrt(link, b, s, "r2", 1.0 / D)
                pool.tensor_tensor(out=xres[s][:, :], in0=xs[s][:, :], in1=yy[s][:, :], op=ALU.add).then_inc(sem("xres4"), 1)
                yield
                inv_sqrt(link, b, s, "z4")
                yield
                pool.wait_ge(sem("x4_ready"), n)
                pool.tensor_tensor(out=xbias[s][:, :], in0=xs[s][:, :], in1=row("bd5"), op=ALU.add).then_inc(sem("xbias5"), 1)
                yield
                inv_sqrt(link, b, s, "z5")
                yield
                inv_sqrt(link, b, s, "z6")
                yield
                finish()

            whole_run(pool, "pool", [q0, q1, q2, q3])

        @block.scalar
        def _(act):
            act.wait_ge(sem("const_loaded"), 16)
            act.activation(ident_r[:, :], row("ident"), ACT.Copy).then_inc(sem("ident_ready"), 1)
            act.activation(pick_r[:, :], row("pick"), ACT.Copy).then_inc(sem("ident_ready"), 1)
            act.wait_ge(sem("ones_set"), 1)

            def move(dst, src, wait, n, signal, func=ACT.Copy, **kw):
                act.wait_ge(sem(wait), n)
                act.activation(dst, src, func, **kw).then_inc(sem(signal), 1)

            def q0(b, n, s):
                p = ps[s]
                move(xt[s][:, :], p[:, 0:D], "x1_turned", n, "x1t_ready")
                yield
                act.wait_ge(sem("qkv1_ready"), n)
                qk = p[:, BANK:BANK + 2 * D].rearrange("p (t h c) -> p t h c", t=2, h=H)
                act.activation(parts(q4[s])[:, :, 0::2, :], qk[:, 0].unsqueeze(2).broadcast_to([128, H, 2, HD]), ACT.Copy)
                act.activation(parts(k4[s])[:, :, 0:2, :], qk[:, 1].unsqueeze(2).broadcast_to([128, H, 2, HD]), ACT.Copy)
                act.activation(by_nine(v9[s]), heads(p[:, BANK + 2 * D:BANK + 3 * D]), ACT.Copy).then_inc(sem("v1_ready"), 1)
                yield
                move(qt[s][:, :], p[:, 0:BANK], "q1_turned", n, "q1t_ready")
                yield
                for half in range(2):
                    move(prob[s][:, 2 * half * BANK:(2 * half + 1) * BANK], p[:, 0:BANK], "a1_ready", b * 2 + half + 1, "p1_act", ACT.Relu, scale=HD ** -0.5)
                    yield
                move(sums[s], p[:, 0:BANK], "o1_summed", n, "o1_moved")
                yield
                move(kt2[s][:, :].rearrange("p (a m) -> p a m", a=2), p[:, :].rearrange("p (a m) -> p a m", a=2)[:, :, 0:4 * C], "k2_ready", n, "k2t_ready")
                yield
                move(heads(v65[s], XH, C)[:, 0:8, 0:XD], heads(p[:, 0:BANK], 8, C), "v2_ready", n, "v2_act")
                yield
                move(xt[s][:, :], p[:, 0:D], "o1_turned", n, "o1t_ready")
                move(kt5[s][:, :], p[:, BANK:BANK + 4 * CE], "k5_turned", n, "k5t_ready")
                yield

            def q1(b, n, s):
                p = ps[s]
                move(xt[s][:, :], p[:, 0:D], "h2_turned", n, "h2t_ready")
                yield
                act.wait_ge(sem("f_used"), n)
                act.wait_ge(sem("q2_ready"), n)
                for k in range(4):
                    r = act.activation(qt2[s][:, k * S:(k + 1) * S], p[:, k * S:(k + 1) * S], ACT.Identity,
                                       scale=fs1[s][:, k:k + 1], bias=fs1[s][:, XB + k:XB + k + 1])
                r.then_inc(sem("q2t_act"), 1)
                yield
                move(nmt[s][:, :], p[:, 0:S], "m2_turned", n, "m2t_ready")
                yield
                for half in range(2):
                    at = slice(2 * half * BANK, 2 * (half + 1) * BANK)
                    move(prob[s][0:C, at], p[0:C, :], "s2t_ready", b * 2 + half + 1, "p2_ready", ACT.Exp, scale=XD ** -0.5)
                    yield
                move(prob[s][:, 0:BANK], p[:, 0:BANK], "o2_turned", n, "o2t_act")
                yield

            def q2(b, n, s):
                p = ps[s]
                move(xt[s][:, :], p[:, 0:D], "x3_turned", n, "x3t_ready")
                yield
                act.wait_ge(sem("lg_max"), n)
                act.activation(big[s][0:E, S:2 * S], big[s][0:E, 0:S], ACT.Exp, bias=esum[s][:, 0:1], accum_out=esum[s][:, 1:2]).then_inc(sem("lg_exp"), 1)
                yield

                def relu(layer, g):
                    act.wait_ge(sem(f"e{layer}_ready"), b * 4 + g + 1)
                    at = g % 2 * BANK
                    for k in range(4):
                        cols = slice(at + k * S, at + (k + 1) * S)
                        e = 4 * g + k
                        r = act.activation(prob[s][:, cols], p[:, cols], ACT.Relu, bias=row(f"b{layer}")[:, e:e + 1])
                    r.then_inc(sem(f"e{layer}_relu"), 1)

                for g in (0, 2):
                    relu(1, g)
                    yield
                    relu(1, g + 1)
                    yield
                    relu(2, g)
                    yield
                    relu(2, g + 1)
                    yield
                move(xt[s][:, :], p[:, 0:D], "h4_turned", n, "h4t_ready")
                yield
                act.wait_ge(sem("rkv4_ready"), n)
                act.activation(oo[s][:, :], p[:, BANK:BANK + D], ACT.Tanh, scale=0.5)
                act.activation(junk[s][:, :], p[:, BANK + D:BANK + 2 * D], ACT.Copy)
                act.activation(by_nine(v9[s]), heads(p[:, BANK + 2 * D:BANK + 3 * D]), ACT.Copy).then_inc(sem("rkv4_moved"), 1)
                yield
                move(qt[s][:, :], p[:, 0:BANK], "r4_turned", n, "r4t_ready")
                yield

            def q3(b, n, s):
                p = ps[s]
                for half in range(2):
                    move(prob[s][:, 2 * half * BANK:(2 * half + 1) * BANK], p[:, 0:BANK], "a4_ready", b * 2 + half + 1, "a4_moved")
                    yield
                move(sums[s], p[:, 0:BANK], "y4_summed", n, "y4_moved")
                yield
                move(xt[s][:, :], p[:, 0:D], "h5_turned", n, "h5t_ready")
                yield
                move(big[s][:, 0:HID], p[:, 0:HID], "up4_ready", n, "tanh_u", ACT.Tanh, scale=0.5)
                yield
                move(xt[s][:, :], p[:, 0:D], "x5_turned", n, "x5t_ready")
                yield
                move(qt[s][:, :], p[:, 0:BANK], "q5_turned", n, "q5t_ready")
                yield
                move(nmt[s][:, :], p[:, 0:S], "m5_turned", n, "m5t_ready")
                yield
                for half in range(2):
                    at = slice(2 * half * BANK, 2 * (half + 1) * BANK)
                    move(prob[s][0:C, at], p[0:C, :], "s5t_ready", b * 2 + half + 1, "p5_ready", ACT.Exp, scale=HD ** -0.5)
                    yield
                move(sums[s], p[:, 0:BANK], "o5_summed", n, "o5_moved")
                yield
                move(xt[s][:, :], p[:, 0:D], "o5_turned", n, "o5t_ready")
                yield
                move(xt[s][:, :], p[:, 0:D], "x6_turned", n, "x6t_ready")
                yield

            whole_run(act, "act", [q0, q1, q2, q3])

        @block.vector
        def _(dve):
            v = nc.vector
            dve.wait_ge(sem("ones_set"), 1)
            dve.wait_ge(sem("const_loaded"), 16)

            def ternary():
                tern, low = weight("tern6"), prob[3][:, 0:D]
                dve.wait_ge(sem(f"w_loaded{len(PIECES) - 1}"), 16)
                v.tensor_reduce(t_abs[:, :], tern, AX.X, ALU.add, apply_absolute_value=True).then_inc(sem("t_abs"), 1)
                dve.wait_ge(sem("t_sum"), 1)
                v.tensor_scalar(t_scale[:, :], ps[3][:, 0:1], 1.0 / (D * D), LN_EPS, ALU.mult, ALU.max).then_inc(sem("t_link"), 1)
                dve.wait_ge(sem("t_link"), 1)
                v.tensor_scalar(t_half[:, :], t_scale[:, :], 0.5, None, ALU.mult)
                v.tensor_scalar(t_neg[:, :], t_scale[:, :], -0.5, None, ALU.mult).then_inc(sem("t_link"), 1)
                dve.wait_ge(sem("t_link"), 2)
                v.tensor_scalar(low, tern, t_neg[:, :], None, ALU.is_lt).then_inc(sem("t_link"), 1)
                dve.wait_ge(sem("t_link"), 3)
                v.scalar_tensor_tensor(tern, tern, t_half[:, :], low, ALU.is_gt, ALU.subtract).then_inc(sem("t_link"), 1)
                dve.wait_ge(sem("t_link"), 4)
                v.tensor_scalar(tern, tern, t_scale[:, :], None, ALU.mult).then_inc(sem("tern_ready"), 1)

            def var(link, z, s, name, rows=128):
                k = LN_AT[name]
                link(v.bn_stats(stats[s][0:rows, :], z), apart=True)
                v.bn_aggr(mv[s][0:rows, 2 * k:2 * k + 2], stats[s][0:rows, :]).then_inc(ln_sem(name, "var"), 1)

            def norm(out_, z, b, s, name, rows=128):
                k = LN_AT[name]
                dve.wait_ge(ln_sem(name, "rstd"), ln_count(name, b))
                return v.tensor_scalar(out_, z, mv[s][0:rows, 2 * k:2 * k + 1], rstd[s][0:rows, k:k + 1], ALU.subtract, ALU.mult)

            def square(t, s, name):
                k = LN_AT[name]
                v.tensor_tensor_reduce(out=junk[s][:, :], in0=t[:, :], in1=t[:, :], scale=1.0, scalar=0.0, op0=ALU.mult, op1=ALU.add,
                                       accum_out=mv[s][:, 2 * k + 1:2 * k + 2]).then_inc(ln_sem(name, "var"), 1)

            def rms(t, b, s, name, w, signal):
                k = LN_AT[name]
                dve.wait_ge(ln_sem(name, "rstd"), ln_count(name, b))
                v.scalar_tensor_tensor(oo[s][:, :], t[:, :], rstd[s][:, k:k + 1], row(w), ALU.mult, ALU.mult).then_inc(sem(signal), 1)

            def weighted(link, p, s, weights, signal):
                link(v.reciprocal(rec[s][:, :], weights))
                v.tensor_tensor(heads(oo[s]), p[:, :, 0:HD], rec[s][:, :].unsqueeze(2).broadcast_to([128, H, HD]), ALU.mult).then_inc(sem(signal), 1)

            def dups(t):
                return t.unsqueeze(2).broadcast_to([t.shape[0], H, 2, HD])

            def row_max(s, half, width, used):
                sc = ps[s][:, :].rearrange("p (a m) -> p a m", a=2)[:, :, 0:4 * width].rearrange("p a (h m) -> p a h m", h=4)[:, :, :, 0:used]
                return v.tensor_reduce(neg_max[s][:, 8 * half:8 * half + 8].rearrange("p (a h) -> p a h", a=2), sc, AX.X, ALU.max, negate=True)

            def split_max(link, s):
                two = nm[s][:, :].rearrange("p (r a h) -> p r a h", r=4, a=2)
                m = neg_max[s][:, :].unsqueeze(1).broadcast_to([128, 4, H])
                link(v.tensor_copy(two[:, :, 0, :], m))
                return v.tensor_tensor(two[:, :, 1, :], m, two[:, :, 0, :].bitcast(F), ALU.subtract)

            def q0(b, n, s):
                p = ps[s]
                link, finish = linker(dve, "dve", 0, b)
                dve.wait_ge(sem(f"x_loaded{s}"), loads(b, s))
                var(link, cin[s][:, :], s, "ctx", C)
                link(norm(yy[s][0:C, :], cin[s][:, :], b, s, "ctx", C))
                link(v.tensor_tensor(yy[s][0:C, :], yy[s][0:C, :], row("ln1_w", C), ALU.mult))
                v.tensor_tensor(yy[s][0:C, :], yy[s][0:C, :], row("ln1_b", C), ALU.add).then_inc(sem("cn_ready"), 1)
                yield
                dve.wait_ge(sem("v1_ready"), n)
                qk = p[:, BANK:BANK + 2 * D].rearrange("p (t h c) -> p t h c", t=2, h=H)
                v.tensor_tensor(parts(q4[s])[:, :, 1::2, :], dups(qk[:, 0]), parts(q4[s])[:, :, 0::2, :].bitcast(F), ALU.subtract)
                v.tensor_tensor(parts(k4[s])[:, :, 2:4, :], dups(qk[:, 1]), parts(k4[s])[:, :, 0:2, :].bitcast(F), ALU.subtract).then_inc(sem("qk1_split"), 1)
                yield
                dve.wait_ge(sem("k1_turned"), n)
                v.tensor_copy(kt[s][:, :], p[:, BANK:2 * BANK]).then_inc(sem("k1t_ready"), 1)
                yield
                dve.wait_ge(sem("c_turned"), n)
                v.tensor_copy(ct[s][:, :], p[:, 0:2 * C]).then_inc(sem("ct_ready"), 1)
                yield
                for half in range(2):
                    dve.wait_ge(sem("a1_ready"), b * 2 + half + 1)
                    v.tensor_scalar(prob[s][:, (2 * half + 1) * BANK:(2 * half + 2) * BANK], p[:, BANK:2 * BANK], HD ** -0.5, 0.0, ALU.mult, ALU.max).then_inc(sem("p1_dve"), 1)
                    yield
                dve.wait_ge(sem("kv5_ready"), n)
                v.tensor_tensor(zz[s][0:C, :], p[0:C, BANK:BANK + D], row("bk5", C), ALU.add).then_inc(sem("kb_ready"), 1)
                v.tensor_tensor(by_nine(v95[s], C), heads(p[:, BANK + D:BANK + 2 * D], rows=C),
                                row("bv5", C).rearrange("p (h c) -> p h c", h=H), ALU.add).then_inc(sem("v5_ready"), 1)
                yield
                dve.wait_ge(sem("o1_ready"), n)
                o = heads(p[:, 0:BANK])
                link(v.tensor_scalar(den[s][:, :], o[:, :, HD], KERN_EPS, None, ALU.add))
                weighted(link, o, s, den[s][:, :], "o1_normed")
                yield
                dve.wait_ge(sem("v2_ready"), n)
                v.tensor_copy(heads(v65[s], XH, C)[:, 8:16, 0:XD], heads(p[:, BANK:2 * BANK], 8, C)).then_inc(sem("v2_dve"), 1)
                yield
                dve.wait_ge(sem("y1_ready"), n)
                dve.wait_ge(sem("x_used"), n)
                link(v.tensor_tensor(yy[s][:, :], p[:, 0:D], xbias[s][:, :], ALU.add))
                var(link, yy[s][:, :], s, "y1")
                yield
                link(norm(yy[s][:, :], yy[s][:, :], b, s, "y1"))
                link(v.tensor_tensor(yy[s][:, :], yy[s][:, :], row("gamma"), ALU.mult))
                link(v.tensor_tensor(zz[s][:, :], yy[s][:, :], xres[s][:, :], ALU.add))
                var(link, zz[s][:, :], s, "z1")
                yield
                link(norm(xs[s][:, :], zz[s][:, :], b, s, "z1"))
                var(link, xs[s][:, :], s, "q2")
                yield
                link(norm(oo[s][:, :], xs[s][:, :], b, s, "q2"))
                link(v.tensor_tensor(oo[s][:, :], oo[s][:, :], row("ln2_w"), ALU.mult))
                v.tensor_tensor(oo[s][:, :], oo[s][:, :], row("ln2_b"), ALU.add).then_inc(sem("h2_ready"), 1)
                yield
                finish()

            def q1(b, n, s):
                p = ps[s]
                link, finish = linker(dve, "dve", 1, b)
                dve.wait_ge(sem("f_used"), n)
                dve.wait_ge(sem("q2_ready"), n)
                for k in range(4, 8):
                    r = v.tensor_scalar(qt2[s][:, k * S:(k + 1) * S], p[:, k * S:(k + 1) * S], fs1[s][:, k:k + 1], fs1[s][:, XB + k:XB + k + 1], ALU.mult, ALU.add)
                r.then_inc(sem("q2t_dve"), 1)
                yield
                dve.wait_ge(sem("s2_ready"), b * 2 + 1)
                row_max(s, 0, C, C).then_inc(sem("m2_first"), 1)
                yield
                dve.wait_ge(sem("s2_ready"), b * 2 + 2)
                link(row_max(s, 1, C, C))
                split_max(link, s).then_inc(sem("m2_split"), 1)
                yield
                for half in range(2):
                    dve.wait_ge(sem("o2_ready"), b * 2 + half + 1)
                    o2 = p[:, :].rearrange("p (a m) -> p a m", a=2)[:, :, 0:4 * 65].rearrange("p a (h m) -> p a h m", h=4)
                    r2 = rec[s][:, 8 * half:8 * half + 8]
                    link(v.reciprocal(r2.rearrange("p (a h) -> p a h", a=2), o2[:, :, :, XD]))
                    for a in range(2):
                        at = (2 * half + a) * 4 * XD
                        r = v.tensor_tensor(heads(big[s][:, at:at + 4 * XD], 4), o2[:, a, :, 0:XD], r2[:, 4 * a:4 * a + 4].unsqueeze(2).broadcast_to([128, 4, XD]), ALU.mult)
                    r.then_inc(sem("o2_normed"), 1)
                    yield
                dve.wait_ge(sem("o2_turned"), n)
                v.tensor_copy(prob[s][:, BANK:2 * BANK], p[:, BANK:2 * BANK]).then_inc(sem("o2t_dve"), 1)
                yield
                dve.wait_ge(sem("y2_ready"), n)
                link(v.tensor_tensor(zz[s][:, :], p[:, 0:D], xs[s][:, :], ALU.add))
                var(link, zz[s][:, :], s, "z2")
                yield
                norm(xs[s][:, :], zz[s][:, :], b, s, "z2").then_inc(sem("x2_ready"), 1)
                yield
                finish()

            def q2(b, n, s):
                p = ps[s]
                link, finish = linker(dve, "dve", 2, b)
                lg, prb, left, gate = (big[s][0:E, k * S:(k + 1) * S] for k in range(4))
                dve.wait_ge(sem("lg_ready"), n)
                link(v.tensor_scalar(lg, p[0:E, BANK:BANK + S], row("bg", E), None, ALU.add))
                v.tensor_reduce(esum[s][:, 0:1], lg, AX.X, ALU.max, negate=True).then_inc(sem("lg_max"), 1)
                yield
                dve.wait_ge(sem("lg_exp"), n)
                link(v.reciprocal(esum[s][:, 2:3], esum[s][:, 1:2]))
                link(v.tensor_scalar(prb, prb, esum[s][:, 2:3], None, ALU.mult), apart=True)
                for r in range(TOPK // 8):
                    src = prb if r == 0 else left
                    link(v.max(top8[s][:, :], src), apart=True)
                    link(v.match_replace(left, top8[s][:, :], src, -1.0), apart=True)
                    yield
                v.scalar_tensor_tensor(gate, left, 0.0, prb, ALU.is_lt, ALU.mult).then_inc(sem("gate_ready"), 1)
                yield
                dve.wait_ge(sem("gate_turned"), n)
                v.tensor_copy(gt[s][:, :], p[:, 0:E]).then_inc(sem("gates_in"), 1)
                dve.wait_ge(sem("gates_in"), n)
                link(v.tensor_tensor(junk[s][:, 0:E], gt[s][:, :], row("b3"), ALU.mult))
                link(v.tensor_reduce(gb[s][:, :], junk[s][:, 0:E], AX.X, ALU.add))
                link(v.tensor_scalar(yy[s][:, :], xs[s][:, :], gb[s][:, :], None, ALU.add))
                yield

                def add(g):
                    dve.wait_ge(sem("e3_ready"), b * 4 + g + 1)
                    for k in range(4):
                        e = 4 * g + k
                        a, y = (yy, zz)[e % 2][s][:, :], p[:, g % 2 * BANK + k * D:g % 2 * BANK + (k + 1) * D]
                        if e == 1:
                            r = v.tensor_scalar(a, y, gt[s][:, e:e + 1], None, ALU.mult)
                        else:
                            r = v.scalar_tensor_tensor(a, y, gt[s][:, e:e + 1], a, ALU.mult, ALU.add)
                        r.then_inc(sem("e3_added"), 1)
                        if e:
                            dve.wait_ge(sem("e3_added"), b * E + e)

                add(0)
                yield
                add(1)
                yield
                add(2)
                yield
                add(3)
                dve.wait_ge(sem("e3_added"), b * E + E)
                link(v.tensor_tensor(zz[s][:, :], yy[s][:, :], zz[s][:, :], ALU.add))
                var(link, zz[s][:, :], s, "z3")
                yield
                link(norm(xs[s][:, :], zz[s][:, :], b, s, "z3"))
                square(xs[s], s, "r1")
                yield
                rms(xs[s], b, s, "r1", "rms1", "h4_ready")
                yield
                dve.wait_ge(sem("rkv4_moved"), n)
                link(v.tensor_scalar(oo[s][:, :], oo[s][:, :], 0.5, 0.5, ALU.mult, ALU.add))
                link(v.tensor_copy(parts(q4[s])[:, :, 0::2, :], dups(heads(oo[s]))))
                v.tensor_tensor(parts(q4[s])[:, :, 1::2, :], dups(heads(oo[s])), parts(q4[s])[:, :, 0::2, :].bitcast(F), ALU.subtract).then_inc(sem("r4_split"), 1)
                yield
                link(v.scalar_tensor_tensor(junk[s][:, :], junk[s][:, :], 0.5, junk[s][:, :], ALU.is_gt, ALU.mult))
                kk = heads(junk[s])
                larger = big[s][:, :].rearrange("p (h i j) -> p h i j", h=H, i=HD)
                yield
                link(v.tensor_tensor(larger, kk.unsqueeze(2).broadcast_to([128, H, HD, HD]), kk.unsqueeze(3).broadcast_to([128, H, HD, HD]), ALU.is_gt))
                yield
                link(v.tensor_reduce(heads(zz[s]), larger, AX.X, ALU.add))
                yield
                link(v.scalar_tensor_tensor(junk[s][:, :], zz[s][:, :], 3.5, junk[s][:, :], ALU.is_lt, ALU.mult))
                link(v.tensor_copy(parts(k4[s])[:, :, 0:2, :], dups(kk)))
                v.tensor_tensor(parts(k4[s])[:, :, 2:4, :], dups(kk), parts(k4[s])[:, :, 0:2, :].bitcast(F), ALU.subtract).then_inc(sem("k4_split"), 1)
                yield
                finish()

            def q3(b, n, s):
                p = ps[s]
                link, finish = linker(dve, "dve", 3, b)
                dve.wait_ge(sem("k4_turned"), n)
                v.tensor_copy(kt[s][:, :], p[:, BANK:2 * BANK]).then_inc(sem("k4t_ready"), 1)
                for half in range(2):
                    dve.wait_ge(sem("a4_ready"), b * 2 + half + 1)
                    v.tensor_tensor(prob[s][:, (2 * half + 1) * BANK:(2 * half + 2) * BANK].rearrange("p (g q) -> p g q", q=S),
                                    p[:, BANK:2 * BANK].rearrange("p (g q) -> p g q", q=S),
                                    row("decay").unsqueeze(1).broadcast_to([128, G4, S]), ALU.mult).then_inc(sem("a4_dve"), 1)
                    yield
                dve.wait_ge(sem("y4_mixed"), n)
                link(v.tensor_tensor(yy[s][:, :], p[:, BANK:BANK + D], xs[s][:, :], ALU.add))
                square(yy[s], s, "r2")
                yield
                rms(yy[s], b, s, "r2", "rms2", "h5_ready")
                yield
                dve.wait_ge(sem("tanh_u"), n)
                hid, mid = big[s][:, 0:HID], big[s][:, HID:2 * HID]
                link(v.scalar_tensor_tensor(hid, hid, 1.0, p[:, 0:HID], ALU.add, ALU.mult))
                v.scalar_tensor_tensor(mid, hid, 0.5, p[:, BANK:2 * BANK], ALU.mult, ALU.mult).then_inc(sem("mid_ready"), 1)
                yield
                dve.wait_ge(sem("down4_ready"), n)
                dve.wait_ge(sem("xres4"), n)
                link(v.tensor_tensor(zz[s][:, :], p[:, 0:D], xres[s][:, :], ALU.add))
                var(link, zz[s][:, :], s, "z4")
                yield
                norm(xs[s][:, :], zz[s][:, :], b, s, "z4").then_inc(sem("x4_ready"), 1)
                yield
                dve.wait_ge(sem("q5_ready"), n)
                link(v.tensor_tensor(oo[s][:, :], p[:, BANK:BANK + D], row("bq5"), ALU.add))
                link(v.tensor_copy(parts(q4[s])[:, :, 0::2, :], dups(heads(oo[s]))))
                v.tensor_tensor(parts(q4[s])[:, :, 1::2, :], dups(heads(oo[s])), parts(q4[s])[:, :, 0::2, :].bitcast(F), ALU.subtract).then_inc(sem("q5_split"), 1)
                yield
                dve.wait_ge(sem("s5_ready"), b * 2 + 1)
                row_max(s, 0, CE, C).then_inc(sem("m5_first"), 1)
                yield
                dve.wait_ge(sem("s5_ready"), b * 2 + 2)
                link(row_max(s, 1, CE, C))
                split_max(link, s).then_inc(sem("m5_split"), 1)
                yield
                dve.wait_ge(sem("o5_ready"), n)
                o = heads(p[:, 0:BANK])
                weighted(link, o, s, o[:, :, HD], "o5_normed")
                yield
                dve.wait_ge(sem("y5_ready"), n)
                dve.wait_ge(sem("xbias5"), n)
                link(v.tensor_tensor(zz[s][:, :], p[:, BANK:BANK + D], xbias[s][:, :], ALU.add))
                var(link, zz[s][:, :], s, "z5")
                yield
                norm(xs[s][:, :], zz[s][:, :], b, s, "z5").then_inc(sem("x5_ready"), 1)
                yield
                dve.wait_ge(sem("y6_ready"), n)
                link(v.tensor_tensor(zz[s][:, :], p[:, BANK:BANK + D], xs[s][:, :], ALU.add))
                var(link, zz[s][:, :], s, "z6")
                yield
                if type(b) is int and b >= B - SLOTS + 1:
                    dve.wait_ge(sem("stored"), 16 * (b - SLOTS + 1))
                norm(res[s][:, :], zz[s][:, :], b, s, "z6").then_inc(sem("out_ready"), 1)
                yield
                finish()

            whole_run(dve, "dve", [q0, q1, q2, q3], ternary)

        @block.tensor
        def _(pe):
            mm = pe.matmul

            def turn(out_, src):
                return pe.transpose(out_, src, row("ident", src.shape[0])[:, 0:src.shape[0]])

            def turn_heads(p, src, rows=128):
                for g in range(G4):
                    r = pe.transpose(p[:, g * rows:(g + 1) * rows].bitcast(R), src[0:rows, g * 128:(g + 1) * 128], ident_r[0:rows, 0:rows])
                return r

            def ready(name, n):
                pe.wait_ge(sem(name), n)

            def piece(name, b):
                if type(b) is int and b == 0:
                    for k in range(PIECES.index(name) + 1):
                        pe.wait_ge(sem(f"w_loaded{k}"), 16)

            def narrow_scores(p, s, half):
                for g in range(G4):
                    for j in range(2):
                        at = slice(32 * (2 * half + j), 32 * (2 * half + j) + 32)
                        c0 = j * BANK + g * S
                        r = mm(p[:, c0:c0 + S], kt[s][at, g * S:(g + 1) * S], qt[s][at, g * S:(g + 1) * S], start=True, stop=True)
                return r

            def narrow_sums(p, s, values, rows, j):
                for g in range(G4):
                    at = (j * 4 + g) * S
                    h = 4 * g + j
                    r = mm(p[32 * j:32 * j + 32, g * S:(g + 1) * S], values[s][0:rows, h * 9:h * 9 + 32], prob[s][0:rows, at:at + S], start=True, stop=True)
                return r

            def turn_sums(p, s):
                for g in range(G4):
                    r = turn(p[:, g * S:(g + 1) * S], sums[s][:, g * S:(g + 1) * S])
                return r

            def add_max(p, s, half):
                for k in range(4):
                    for a in range(2):
                        i = (2 * half + a) * 4 + k
                        at = slice(32 * (2 * half + a), 32 * (2 * half + a) + 32)
                        r = mm(p[0:C, a * BANK + k * S:a * BANK + (k + 1) * S], pick_r[at, i:i + 1].broadcast_to([32, C]), nmt[s][at, :],
                               start=False, stop=(k == 3), skip_group_check=True)
                return r

            ready("ident_ready", 2)
            ready("ones_set", 1)

            def ternary():
                ready("t_abs", 1)
                mm(ps[3][:, 0:1], v9_ones, t_abs[:, :], start=True, stop=True).then_inc(sem("t_sum"), 1)

            v9_ones = v9[3][:, 8:9].broadcast_to([128, 128])

            def q0(b, n, s):
                p = ps[s]
                ready(f"x_loaded{s}", loads(b, s))
                turn(p[:, 0:D], xin[s][:, :]).then_inc(sem("x1_turned"), 1)
                yield
                piece("qkv1", b)
                ready("x1t_ready", n)
                mm(p[:, BANK:BANK + 3 * D], xt[s][:, :], weight("qkv1"), start=True, stop=True).then_inc(sem("qkv1_ready"), 1)
                yield
                ready("qk1_split", n)
                turn_heads(p[:, 0:BANK], q4[s]).then_inc(sem("q1_turned"), 1)
                turn_heads(p[:, BANK:2 * BANK], k4[s]).then_inc(sem("k1_turned"), 1)
                yield
                ready("q1t_ready", n)
                ready("cn_ready", n)
                turn(p[:, 0:C], yy[s][0:C, :])
                turn(p[:, C:2 * C], cin[s][:, :]).then_inc(sem("c_turned"), 1)
                yield
                ready("k1t_ready", n)
                ready("ct_ready", n)
                narrow_scores(p, s, 0).then_inc(sem("a1_ready"), 1)
                yield
                ready("p1_act", b * 2 + 1)
                ready("p1_dve", b * 2 + 1)
                narrow_scores(p, s, 1).then_inc(sem("a1_ready"), 1)
                yield
                piece("out1", b)
                ready("p1_act", b * 2 + 2)
                ready("p1_dve", b * 2 + 2)
                for j in range(4):
                    r = narrow_sums(p, s, v9, 128, j)
                    if j < 3:
                        yield
                r.then_inc(sem("o1_summed"), 1)
                yield
                mm(p[0:C, BANK:BANK + 2 * D], ct[s][:, C:2 * C], weight("kv5"), start=True, stop=True).then_inc(sem("kv5_ready"), 1)
                yield
                ready("o1_moved", n)
                turn_sums(p, s).then_inc(sem("o1_ready"), 1)
                yield
                ready("o1_normed", n)
                ready("v5_ready", n)
                for k in range(XB):
                    at = k // 4 * BANK + k % 4 * C
                    r = mm(p[:, at:at + C], weight("k2", k * 128, (k + 1) * 128), ct[s][:, 0:C], start=True, stop=True)
                    if k == 3:
                        yield
                r.then_inc(sem("k2_ready"), 1)
                yield
                ready("k2t_ready", n)
                for k in range(2):
                    r = mm(p[0:C, k * BANK:(k + 1) * BANK], ct[s][:, 0:C], weight("v2", k * BANK, (k + 1) * BANK), start=True, stop=True)
                    if k == 0:
                        yield
                r.then_inc(sem("v2_ready"), 1)
                yield
                ready("v2_act", n)
                turn(p[:, 0:D], oo[s][:, :]).then_inc(sem("o1_turned"), 1)
                ready("v2_dve", n)
                ready("k5_split", n)
                turn_heads(p[:, BANK:2 * BANK], k4[s], CE).then_inc(sem("k5_turned"), 1)
                yield
                ready("o1t_ready", n)
                mm(p[:, 0:D], xt[s][:, :], weight("out1"), start=True, stop=True).then_inc(sem("y1_ready"), 1)
                yield

            def q1(b, n, s):
                p = ps[s]
                piece("out2", b)
                ready("h2_ready", n)
                turn(p[:, 0:D], oo[s][:, :]).then_inc(sem("h2_turned"), 1)
                yield
                ready("h2t_ready", n)
                ready("k5t_ready", n)
                for k in range(XB):
                    r = mm(p[:, k * S:(k + 1) * S], weight("q2", k * 128, (k + 1) * 128), xt[s][:, :], start=True, stop=True)
                    if k == 3:
                        yield
                r.then_inc(sem("q2_ready"), 1)
                yield
                ready("q2t_act", n)
                ready("q2t_dve", n)
                for half in range(2):
                    if half == 1:
                        ready("m2_first", n)
                    for k in range(4 * half, 4 * half + 4):
                        for par in range(2):
                            at = slice(64 * par, 64 * par + 64)
                            c0 = par * BANK + k % 4 * C
                            r = mm(p[:, c0:c0 + C], qt2[s][at, k * S:(k + 1) * S], kt2[s][at, k * C:(k + 1) * C], start=True, stop=True)
                    r.then_inc(sem("s2_ready"), 1)
                    yield
                ready("m2_split", n)
                turn_max = pe.transpose(p[:, 0:S].bitcast(R), nm[s][:, :], ident_r[:, :])
                turn_max.then_inc(sem("m2_turned"), 1)
                yield
                ready("m2t_ready", n)
                for half in range(2):
                    if half == 1:
                        ready("p2_ready", b * 2 + 1)
                    for k in range(4 * half, 4 * half + 4):
                        for par in range(2):
                            at = slice(64 * par, 64 * par + 64)
                            c0 = par * BANK + k % 4 * S
                            mm(p[0:C, c0:c0 + S], kt2[s][at, k * C:(k + 1) * C], qt2[s][at, k * S:(k + 1) * S], start=(k % 4 == 0), stop=False, skip_group_check=True)
                    add_max(p, s, half).then_inc(sem("s2t_ready"), 1)
                    yield
                ready("p2_ready", b * 2 + 2)
                for half in range(2):
                    if half == 1:
                        ready("o2_normed", b * 2 + 1)
                    for i in range(8 * half, 8 * half + 8):
                        h = 2 * (i // 8 * 4 + i % 4) + i // 4 % 2
                        o0 = i // 4 % 2 * BANK + i % 4 * 65
                        r = mm(p[:, o0:o0 + 65], prob[s][0:C, i * S:(i + 1) * S], v65[s][:, h * 65:(h + 1) * 65], start=True, stop=True)
                    r.then_inc(sem("o2_ready"), 1)
                    yield
                ready("o2_normed", b * 2 + 2)
                for k in range(XB):
                    r = turn(p[:, k * S:(k + 1) * S], big[s][:, k * 128:(k + 1) * 128])
                    if k == 3:
                        yield
                r.then_inc(sem("o2_turned"), 1)
                yield
                ready("o2t_act", n)
                ready("o2t_dve", n)
                for k in range(XB):
                    r = mm(p[:, 0:D], prob[s][:, k * S:(k + 1) * S], weight("out2", k * D, (k + 1) * D), start=(k == 0), stop=(k == XB - 1))
                    if k == 3:
                        yield
                r.then_inc(sem("y2_ready"), 1)
                yield

            def q2(b, n, s):
                p = ps[s]
                piece("exp1", b)
                ready("x2_ready", n)
                turn(p[:, 0:D], xs[s][:, :]).then_inc(sem("x3_turned"), 1)
                yield
                ready("x3t_ready", n)
                mm(p[0:E, BANK:BANK + S], weight("gate"), xt[s][:, :], start=True, stop=True).then_inc(sem("lg_ready"), 1)
                yield

                def layer(k, g):
                    for e in range(4 * g, 4 * g + 4):
                        c0 = g % 2 * BANK + e % 4 * S
                        w = weight(f"exp{k}", e * D, (e + 1) * D)
                        if k == 1:
                            r = mm(p[:, c0:c0 + S], w, xt[s][:, :], start=True, stop=True)
                        elif k == 2:
                            r = mm(p[:, c0:c0 + S], w, prob[s][:, c0:c0 + S], start=True, stop=True)
                        else:
                            r = mm(p[:, c0:c0 + S], prob[s][:, c0:c0 + S], w, start=True, stop=True)
                    r.then_inc(sem(f"e{k}_ready"), 1)

                for g in (0, 2):
                    if g == 2:
                        ready("e3_added", b * E + 4)
                    layer(1, g)
                    yield
                    if g == 0:
                        ready("lg_max", n)
                    else:
                        ready("e3_added", b * E + 8)
                    layer(1, g + 1)
                    yield
                    if g == 0:
                        piece("exp3", b)
                    ready("e1_relu", b * 4 + g + 1)
                    layer(2, g)
                    yield
                    ready("e1_relu", b * 4 + g + 2)
                    layer(2, g + 1)
                    yield
                    wait_apart(pe, sem("e2_relu"), b * 4 + g + 1)
                    if g == 0:
                        wait_apart(pe, sem("gate_ready"), n)
                        turn(p[:, 0:E], big[s][0:E, 3 * S:4 * S]).then_inc(sem("gate_turned"), 1)
                        yield
                        ready("gates_in", n)
                    layer(3, g)
                    yield
                    ready("e2_relu", b * 4 + g + 2)
                    layer(3, g + 1)
                    yield
                piece("tern6", b)
                yield
                ready("h4_ready", n)
                turn(p[:, 0:D], oo[s][:, :]).then_inc(sem("h4_turned"), 1)
                yield
                ready("h4t_ready", n)
                mm(p[:, BANK:BANK + 3 * D], xt[s][:, :], weight("rkv4"), start=True, stop=True).then_inc(sem("rkv4_ready"), 1)
                yield
                ready("r4_split", n)
                turn_heads(p[:, 0:BANK], q4[s]).then_inc(sem("r4_turned"), 1)
                yield
                ready("k4_split", n)
                turn_heads(p[:, BANK:2 * BANK], k4[s]).then_inc(sem("k4_turned"), 1)
                yield

            def q3(b, n, s):
                p = ps[s]
                ready("r4t_ready", n)
                ready("k4t_ready", n)
                narrow_scores(p, s, 0).then_inc(sem("a4_ready"), 1)
                yield
                ready("a4_moved", b * 2 + 1)
                ready("a4_dve", b * 2 + 1)
                narrow_scores(p, s, 1).then_inc(sem("a4_ready"), 1)
                yield
                ready("a4_decayed", b * 2 + 2)
                ready("a4_dve", b * 2 + 2)
                for j in range(4):
                    r = narrow_sums(p, s, v9, 128, j)
                    if j < 3:
                        yield
                r.then_inc(sem("y4_summed"), 1)
                yield
                ready("y4_moved", n)
                for g in range(G4):
                    r = mm(p[:, BANK:BANK + D], sums[s][:, g * S:(g + 1) * S], weight("out4", g * D, (g + 1) * D), start=(g == 0), stop=(g == G4 - 1))
                r.then_inc(sem("y4_mixed"), 1)
                yield
                ready("h5_ready", n)
                turn(p[:, 0:D], oo[s][:, :]).then_inc(sem("h5_turned"), 1)
                yield
                ready("h5t_ready", n)
                for k in range(8):
                    r = mm(p[:, k * S:(k + 1) * S], weight("up4", k * 128, (k + 1) * 128), xt[s][:, :], start=True, stop=True)
                    if k == 3:
                        yield
                r.then_inc(sem("up4_ready"), 1)
                yield
                ready("mid_ready", n)
                for k in range(4):
                    r = mm(p[:, 0:D], big[s][:, HID + k * S:HID + (k + 1) * S], weight("down4", k * D, (k + 1) * D), start=(k == 0), stop=(k == 3))
                r.then_inc(sem("down4_ready"), 1)
                yield
                ready("x4_ready", n)
                turn(p[:, 0:D], xs[s][:, :]).then_inc(sem("x5_turned"), 1)
                yield
                ready("x5t_ready", n)
                mm(p[:, BANK:BANK + D], xt[s][:, :], weight("q5"), start=True, stop=True).then_inc(sem("q5_ready"), 1)
                yield
                ready("q5_split", n)
                turn_heads(p[:, 0:BANK], q4[s]).then_inc(sem("q5_turned"), 1)
                yield
                ready("q5t_ready", n)
                for half in range(2):
                    if half == 1:
                        ready("m5_first", n)
                    for g in range(G4):
                        for j in range(2):
                            at = slice(32 * (2 * half + j), 32 * (2 * half + j) + 32)
                            c0 = j * BANK + g * CE
                            r = mm(p[:, c0:c0 + CE], qt[s][at, g * S:(g + 1) * S], kt5[s][at, g * CE:(g + 1) * CE], start=True, stop=True)
                    r.then_inc(sem("s5_ready"), 1)
                    yield
                ready("m5_split", n)
                turn_max = pe.transpose(p[:, 0:S].bitcast(R), nm[s][:, :], ident_r[:, :])
                turn_max.then_inc(sem("m5_turned"), 1)
                yield
                ready("m5t_ready", n)
                for half in range(2):
                    if half == 1:
                        ready("p5_ready", b * 2 + 1)
                    for g in range(G4):
                        for j in range(2):
                            at = slice(32 * (2 * half + j), 32 * (2 * half + j) + 32)
                            c0 = j * BANK + g * S
                            mm(p[0:C, c0:c0 + S], kt5[s][at, g * CE:g * CE + C], qt[s][at, g * S:(g + 1) * S], start=(g == 0), stop=False, skip_group_check=True)
                    add_max(p, s, half).then_inc(sem("s5t_ready"), 1)
                    yield
                ready("p5_ready", b * 2 + 2)
                for j in range(4):
                    r = narrow_sums(p, s, v95, C, j)
                    if j < 3:
                        yield
                r.then_inc(sem("o5_summed"), 1)
                yield
                ready("o5_moved", n)
                turn_sums(p, s).then_inc(sem("o5_ready"), 1)
                yield
                ready("o5_normed", n)
                turn(p[:, 0:D], oo[s][:, :]).then_inc(sem("o5_turned"), 1)
                yield
                ready("o5t_ready", n)
                mm(p[:, BANK:BANK + D], xt[s][:, :], weight("out5"), start=True, stop=True).then_inc(sem("y5_ready"), 1)
                yield
                if type(b) is int and b == 0:
                    ready("tern_ready", 1)
                ready("x5_ready", n)
                turn(p[:, 0:D], xs[s][:, :]).then_inc(sem("x6_turned"), 1)
                yield
                ready("x6t_ready", n)
                mm(p[:, BANK:BANK + D], xt[s][:, :], weight("tern6"), start=True, stop=True).then_inc(sem("y6_ready"), 1)
                yield

            def before_last_quarters():
                ternary()
                ready("tern_ready", 1)

            whole_run(pe, "pe", [q0, q1, q2, q3], before_last_quarters)


def kernel(**inputs):
    import concourse.bacc as bacc
    from concourse.bass_utils import run_bass_kernel_spmd

    a = {k: np.asarray(v) for k, v in inputs.items()}
    f = np.float32

    def heads_apart(w, parts):
        return w.reshape(D, H, parts, HD).transpose(0, 2, 1, 3).reshape(D, parts * D)

    kv = a["L0_xattn_Wkv"]
    experts = lambda w: w.transpose(1, 0, 2).reshape(D, E * D)
    out2 = a["L0_xattn_Wout"].reshape(2, 4, 2, XD, D).transpose(0, 2, 1, 3, 4).reshape(XB, 128, D).transpose(1, 0, 2).reshape(128, XB * D)
    out4 = np.zeros((4, 32, G4, D), f)
    out4[:, :HD] = a["L1_attn_Wo"].reshape(G4, 4, HD, D).transpose(1, 2, 0, 3)
    out4 = out4.reshape(128, G4 * D)
    weights = dict(
        qkv1=heads_apart(a["L0_attn_w_qkv"], 3), k2=kv[:, :XH * XD], v2=kv[:, XH * XD:],
        kv5=np.concatenate([a["L1_xattn_wk_w"].T, a["L1_xattn_wv_w"].T], 1), q2=a["L0_xattn_Wq"],
        gate=a["L0_ffn_Wg"], exp1=experts(a["L0_ffn_w1"]), exp2=experts(a["L0_ffn_w2"]), exp3=experts(a["L0_ffn_w3"]),
        rkv4=np.concatenate([a["L1_attn_Wr"], a["L1_attn_Wk"], a["L1_attn_Wv"]], 1),
        up4=np.concatenate([a["L1_attn_w1"], a["L1_attn_w2"]], 1), q5=a["L1_xattn_wq_w"].T,
        out1=a["L0_attn_w_out"], out2=out2, out4=out4,
        down4=a["L1_attn_w3"].reshape(4, 128, D).transpose(1, 0, 2).reshape(128, HID), out5=a["L1_xattn_dense_w"].T,
        tern6=a["L1_ffn_weight"].T)
    t = np.arange(S)
    lag = t[None, :] - t[:, None]
    decay = np.where(lag >= 0, DECAY ** np.maximum(lag, 0).astype(np.float64), 0.0).astype(f)
    pick = np.tile(np.eye(XH, dtype=f), (8, 1))
    rows = lambda v: np.broadcast_to(v.reshape(1, -1), (128, v.size))
    const = dict(
        ident=np.eye(128, dtype=f), decay=decay, pick=pick, b_out=rows(a["L0_attn_b_out"]), gamma=rows(a["L0_attn_gamma"]),
        beta=rows(a["L0_attn_beta"]), ln1_w=rows(a["L0_xattn_ln1_w"]), ln1_b=rows(a["L0_xattn_ln1_b"]), ln2_w=rows(a["L0_xattn_ln2_w"]),
        ln2_b=rows(a["L0_xattn_ln2_b"]), rms1=rows(a["L1_attn_norm1_w"]), rms2=rows(a["L1_attn_norm2_w"]), bk5=rows(a["L1_xattn_wk_b"]),
        bv5=rows(a["L1_xattn_wv_b"]), bq5=rows(a["L1_xattn_wq_b"]), bd5=rows(a["L1_xattn_dense_b"]), b1=rows(a["L0_ffn_b1"]),
        b2=rows(a["L0_ffn_b2"]), b3=rows(a["L0_ffn_b3"]),
        bg=np.concatenate([a["L0_ffn_bg"].reshape(E, 1), np.zeros((D - E, 1), f)], 0))
    fs = a["fside_Bx16_0"].reshape(B, XB, 2)
    fs = np.repeat(fs.transpose(0, 2, 1), XD, axis=1)
    ctx = np.concatenate([a["ctx_1024"], np.zeros((B, S - C, D), f)], 1)
    arrays = {
        "rows_in": np.concatenate([a["x"], ctx, fs], 2), "weights": np.concatenate([weights[n] for n, _ in WEIGHTS], 1),
        "const": np.concatenate([const[n] for n, _ in CONST], 1),
    }
    arrays = {k: np.ascontiguousarray(v) for k, v in arrays.items()}
    nc = bacc.Bacc("TRN2", target_bir_lowering=False, num_devices=1)
    args = [nc.dram_tensor(k, v.shape, mybir.dt.float32, kind="ExternalInput").ap() for k, v in arrays.items()]
    out = nc.dram_tensor("decoded", (B, S, D), mybir.dt.float32, kind="ExternalOutput").ap()
    decoder(nc, *args, out)
    r = run_bass_kernel_spmd(nc, [arrays], core_ids=[0])
    return r.results[0]["decoded"]
```
